# Optimizing a Trainium2 kernel written in Bass

```python
import numpy as np
import jax
import jax.numpy as jnp

def _softmax(x, axis=-1):
    return jax.nn.softmax(x, axis=axis)

def _gelu(x):
    return jax.nn.gelu(x, approximate=True)

def _silu(x):
    return jax.nn.silu(x)

def _sigmoid(x):
    return jax.nn.sigmoid(x)

def _layernorm(x, axis=-1, eps=1e-05):
    m = jnp.mean(x, axis=axis, keepdims=True)
    v = jnp.var(x, axis=axis, keepdims=True)
    return (x - m) / jnp.sqrt(v + eps)

def _scatter_add(tgt, idx, src, axis=0):
    return tgt.at[idx].add(src)

def _segment_sum(src, seg, n):
    return jax.ops.segment_sum(src, seg, n)
kernel_name = 'mk_decoder_postln_d1_seqx_r8_f3acb7'

def setup_inputs(seed: int=0):
    np.random.seed(seed)
    _w = jnp.asarray

    def _rec_inputs():
        import jax
        import jax.numpy as jnp
        _rk = jax.random.key(seed)
        x = 7.22e-05 + 1 * jax.random.normal(jax.random.fold_in(_rk, 1), (4, 256, 256), jnp.float32)
        _lenS = 256 - jax.random.randint(jax.random.fold_in(_rk, 7), (4,), 0, max(1, 256 // 4) + 1, jnp.int32)
        _lenS2 = 256 - jax.random.randint(jax.random.fold_in(_rk, 8), (4,), 0, max(1, 256 // 4) + 1, jnp.int32)
        _ctx_1024P = jax.random.normal(jax.random.fold_in(_rk, 11), (4, 16, 128), jnp.float32)
        _ctx_1024c = jax.random.dirichlet(jax.random.fold_in(_rk, 511), 0.3 * jnp.ones((16,), jnp.float32), (4, 256))
        _ctx_1024t = jnp.einsum('bsk,bkd->bsd', _ctx_1024c, _ctx_1024P)
        _ctx_1024t = _ctx_1024t * jax.lax.rsqrt(jnp.mean(jnp.square(_ctx_1024t)) + 1e-12) * 0.953939
        ctx_1024 = 2.81802e-05 + 1.00001 * (_ctx_1024t + 0.3 * jax.random.normal(jax.random.fold_in(_rk, 611), (4, 256, 128), jnp.float32))
        return (x, ctx_1024)
    x, ctx_1024 = _rec_inputs()

    def _L0_attn_setup():
        import jax, jax.numpy as jnp
        import numpy as np
        import math
        EMBED_DIM = 256
        NUM_HEADS = 16
        DEPTH = 12
        HEAD_DIM = EMBED_DIM // NUM_HEADS // 2
        LAMBDA_INIT = 0.8 - 0.6 * math.exp(-0.3 * DEPTH)

        def _diff_attn(query, Wq, Wk, Wv, Wo, lq1, lk1, lq2, lk2, g):
            B, T, E = query.shape
            H, D = (NUM_HEADS, HEAD_DIM)
            S = T
            scaling = D ** (-0.5)
            q = (query @ Wq.T).reshape(B, T, 2 * H, D).transpose(0, 2, 1, 3)
            k = (query @ Wk.T).reshape(B, S, 2 * H, D).transpose(0, 2, 1, 3)
            v = (query @ Wv.T).reshape(B, S, H, 2 * D).transpose(0, 2, 1, 3)
            q = q * scaling
            attn = jnp.einsum('bhtd,bhsd->bhts', q, k)
            attn = jnp.nan_to_num(attn)
            causal = jnp.triu(jnp.full((T, S), -jnp.inf, attn.dtype), k=1)
            attn = jax.nn.softmax(attn + causal, axis=-1)
            lam1 = jnp.exp(jnp.sum(lq1 * lk1))
            lam2 = jnp.exp(jnp.sum(lq2 * lk2))
            lam = lam1 - lam2 + LAMBDA_INIT
            attn = attn.reshape(B, H, 2, T, S)
            attn = attn[:, :, 0] - lam * attn[:, :, 1]
            out = jnp.einsum('bhts,bhsd->bhtd', attn, v)
            rms = jax.lax.rsqrt(jnp.mean(out * out, axis=-1, keepdims=True) + 1e-05)
            out = out * rms * g
            out = out * (1.0 - LAMBDA_INIT)
            out = out.transpose(0, 2, 1, 3).reshape(B, T, H * 2 * D)
            return out @ Wo.T
        key = jax.random.key(seed)
        ks = jax.random.split(key, 9)
        B, T, E = (2, 256, EMBED_DIM)
        s = 1.0 / math.sqrt(E)
        return {'query': jax.random.normal(ks[0], (B, T, E), jnp.float32), 'Wq': jax.random.normal(ks[1], (E, E), jnp.float32) * s, 'Wk': jax.random.normal(ks[2], (E, E), jnp.float32) * s, 'Wv': jax.random.normal(ks[3], (E, E), jnp.float32) * s, 'Wo': jax.random.normal(ks[4], (E, E), jnp.float32) * s, 'lambda_q1': jax.random.normal(ks[5], (HEAD_DIM,), jnp.float32) * 0.1, 'lambda_k1': jax.random.normal(ks[6], (HEAD_DIM,), jnp.float32) * 0.1, 'lambda_q2': jax.random.normal(ks[7], (HEAD_DIM,), jnp.float32) * 0.1, 'lambda_k2': jax.random.normal(ks[8], (HEAD_DIM,), jnp.float32) * 0.1, 'subln_weight': jnp.ones((2 * HEAD_DIM,), jnp.float32)}
    _L0_attn_all = _L0_attn_setup()
    _L0_attn_in = {k: v for k, v in _L0_attn_all.items() if k in ('Wq', 'Wk', 'Wv', 'Wo', 'lambda_q1', 'lambda_k1', 'lambda_q2', 'lambda_k2', 'subln_weight')}
    del _L0_attn_all

    def _L0_xattn_setup():
        import jax, jax.numpy as jnp
        import numpy as np
        key = jax.random.key(seed)
        ks = jax.random.split(key, 6)
        B, L, N, C, D = (8, 64, 256, 128, 128)
        return {'teacher_logits': jax.random.normal(ks[0], (B, L, N), dtype=jnp.float32), 'teacher_features': jax.random.normal(ks[1], (B, N, C), dtype=jnp.float32), 'Wq': jax.random.normal(ks[2], (D, C), dtype=jnp.float32) * (1.0 / np.sqrt(C)), 'bq': jnp.zeros((D,), dtype=jnp.float32), 'Wk': jax.random.normal(ks[3], (D, C), dtype=jnp.float32) * (1.0 / np.sqrt(C)), 'bk': jnp.zeros((D,), dtype=jnp.float32)}
    _L0_xattn_all = _L0_xattn_setup()
    _L0_xattn_in = {k: v for k, v in _L0_xattn_all.items() if k in ('Wq', 'bq', 'Wk', 'bk')}
    del _L0_xattn_all

    def _L0_ffn_setup():
        import jax, jax.numpy as jnp
        import numpy as np
        DIM_IN = 256
        DIM_HIDDEN = 1024
        key = jax.random.key(seed)
        k_x, k_g, k_u, k_d = jax.random.split(key, 4)
        s_in = 1.0 / np.sqrt(DIM_IN)
        s_hid = 1.0 / np.sqrt(DIM_HIDDEN)
        x = jax.random.normal(k_x, (4, 256, DIM_IN), dtype=jnp.float32)
        w_gate = jax.random.uniform(k_g, (DIM_HIDDEN, DIM_IN), jnp.float32, -s_in, s_in)
        w_up = jax.random.uniform(k_u, (DIM_HIDDEN, DIM_IN), jnp.float32, -s_in, s_in)
        w_down = jax.random.uniform(k_d, (DIM_IN, DIM_HIDDEN), jnp.float32, -s_hid, s_hid)
        return {'x': x, 'w_gate': w_gate, 'w_up': w_up, 'w_down': w_down}
    _L0_ffn_all = _L0_ffn_setup()
    _L0_ffn_in = {k: v for k, v in _L0_ffn_all.items() if k in ('w_gate', 'w_up', 'w_down')}
    del _L0_ffn_all
    return {'x': x, 'ctx_1024': ctx_1024, 'L0_attn_Wq': _L0_attn_in['Wq'], 'L0_attn_Wk': _L0_attn_in['Wk'], 'L0_attn_Wv': _L0_attn_in['Wv'], 'L0_attn_Wo': _L0_attn_in['Wo'], 'L0_attn_lambda_q1': _L0_attn_in['lambda_q1'], 'L0_attn_lambda_k1': _L0_attn_in['lambda_k1'], 'L0_attn_lambda_q2': _L0_attn_in['lambda_q2'], 'L0_attn_lambda_k2': _L0_attn_in['lambda_k2'], 'L0_attn_subln_weight': _L0_attn_in['subln_weight'], 'L0_xattn_Wq': _L0_xattn_in['Wq'], 'L0_xattn_bq': _L0_xattn_in['bq'], 'L0_xattn_Wk': _L0_xattn_in['Wk'], 'L0_xattn_bk': _L0_xattn_in['bk'], 'L0_ffn_w_gate': _L0_ffn_in['w_gate'], 'L0_ffn_w_up': _L0_ffn_in['w_up'], 'L0_ffn_w_down': _L0_ffn_in['w_down']}

def reference(x, ctx_1024, L0_attn_Wq, L0_attn_Wk, L0_attn_Wv, L0_attn_Wo, L0_attn_lambda_q1, L0_attn_lambda_k1, L0_attn_lambda_q2, L0_attn_lambda_k2, L0_attn_subln_weight, L0_xattn_Wq, L0_xattn_bq, L0_xattn_Wk, L0_xattn_bk, L0_ffn_w_gate, L0_ffn_w_up, L0_ffn_w_down):
    import jax
    import jax.numpy as jnp

    def _L0_attn_ref(query, Wq, Wk, Wv, Wo, lambda_q1, lambda_k1, lambda_q2, lambda_k2, subln_weight):
        import jax, jax.numpy as jnp
        import numpy as np
        import math
        EMBED_DIM = 256
        NUM_HEADS = 16
        DEPTH = 12
        HEAD_DIM = EMBED_DIM // NUM_HEADS // 2
        LAMBDA_INIT = 0.8 - 0.6 * math.exp(-0.3 * DEPTH)

        def _diff_attn(query, Wq, Wk, Wv, Wo, lq1, lk1, lq2, lk2, g):
            B, T, E = query.shape
            H, D = (NUM_HEADS, HEAD_DIM)
            S = T
            scaling = D ** (-0.5)
            q = (query @ Wq.T).reshape(B, T, 2 * H, D).transpose(0, 2, 1, 3)
            k = (query @ Wk.T).reshape(B, S, 2 * H, D).transpose(0, 2, 1, 3)
            v = (query @ Wv.T).reshape(B, S, H, 2 * D).transpose(0, 2, 1, 3)
            q = q * scaling
            attn = jnp.einsum('bhtd,bhsd->bhts', q, k)
            attn = jnp.nan_to_num(attn)
            causal = jnp.triu(jnp.full((T, S), -jnp.inf, attn.dtype), k=1)
            attn = jax.nn.softmax(attn + causal, axis=-1)
            lam1 = jnp.exp(jnp.sum(lq1 * lk1))
            lam2 = jnp.exp(jnp.sum(lq2 * lk2))
            lam = lam1 - lam2 + LAMBDA_INIT
            attn = attn.reshape(B, H, 2, T, S)
            attn = attn[:, :, 0] - lam * attn[:, :, 1]
            out = jnp.einsum('bhts,bhsd->bhtd', attn, v)
            rms = jax.lax.rsqrt(jnp.mean(out * out, axis=-1, keepdims=True) + 1e-05)
            out = out * rms * g
            out = out * (1.0 - LAMBDA_INIT)
            out = out.transpose(0, 2, 1, 3).reshape(B, T, H * 2 * D)
            return out @ Wo.T
        return _diff_attn(query, Wq, Wk, Wv, Wo, lambda_q1, lambda_k1, lambda_q2, lambda_k2, subln_weight)

    def _L0_xattn_ref(teacher_logits, teacher_features, Wq, bq, Wk, bk):
        import jax, jax.numpy as jnp
        import numpy as np
        query = jnp.einsum('bnc,dc->bnd', teacher_features, Wq) + bq
        key = jnp.einsum('bnc,dc->bnd', teacher_features, Wk) + bk
        energy = jnp.einsum('bnd,bmd->bnm', query, key)
        attention = jax.nn.softmax(energy, axis=-1)
        x_m = jnp.einsum('bln,bmn->blm', teacher_logits, attention)
        return x_m

    def _L0_ffn_ref(x, w_gate, w_up, w_down):
        import jax, jax.numpy as jnp
        import numpy as np
        DIM_IN = 256
        DIM_HIDDEN = 1024
        gate = jnp.einsum('bsd,hd->bsh', x, w_gate)
        up = jnp.einsum('bsd,hd->bsh', x, w_up)
        gated = jax.nn.silu(gate) * up
        return jnp.einsum('bsh,dh->bsd', gated, w_down)
    x = _layernorm(x + _L0_attn_ref(x, L0_attn_Wq, L0_attn_Wk, L0_attn_Wv, L0_attn_Wo, L0_attn_lambda_q1, L0_attn_lambda_k1, L0_attn_lambda_q2, L0_attn_lambda_k2, L0_attn_subln_weight), axis=-1)
    x = _layernorm(x + _L0_xattn_ref(x, ctx_1024, L0_xattn_Wq, L0_xattn_bq, L0_xattn_Wk, L0_xattn_bk), axis=-1)
    x = _layernorm(x + _L0_ffn_ref(x, L0_ffn_w_gate, L0_ffn_w_up, L0_ffn_w_down), axis=-1)
    return x

_drawn_inputs = setup_inputs


def setup_inputs(seed=0):
    import zlib

    import numpy as np

    out = dict(_drawn_inputs(seed))
    spreads = {'L0_attn_subln_weight': (1.0, 0.2), 'L0_xattn_bq': (0.0, 0.1), 'L0_xattn_bk': (0.0, 2.0)}
    factors = {'L0_attn_lambda_q1': 8.0,
     'L0_attn_lambda_k1': 8.0,
     'L0_attn_lambda_q2': 27.384,
     'L0_attn_lambda_k2': 17.508}
    for name, (base, spread) in spreads.items():
        noise = np.random.default_rng([zlib.crc32(name.encode()), seed]).standard_normal(out[name].shape)
        drawn = base * np.exp(spread * noise) if base else spread * noise
        out[name] = jnp.asarray(drawn.astype(out[name].dtype))
    for name, factor in factors.items():
        out[name] = (out[name] * factor).astype(out[name].dtype)
    return out
```

```python
import math
from contextlib import ExitStack

import concourse.bass as bass
from concourse import mybir
from concourse.alu_op_type import AluOpType as ALU

ACT = mybir.ActivationFunctionType
AX = mybir.AxisListType
F32 = mybir.dt.float32
BF16 = mybir.dt.bfloat16
U32 = mybir.dt.uint32

P = 128
B, T, E = 4, 256, 256
TB, EB = T // P, E // P
H = 16
N2 = 2 * H
D = E // N2
DV = 2 * D
HALF = N2 // 2
C = 128
F = 1024
FB = F // P
PARTS = 3
PAIRS = ((0, 0), (0, 1), (1, 0), (1, 1), (0, 2), (2, 0))
M_ROW = D * len(PAIRS)
QUADS = H // 4
RING = 8
LAMBDA_INIT = 0.8 - 0.6 * math.exp(-0.3 * 12)
SCALING = D ** -0.5
EPS = 1e-5
MASKED = -3.0e38
LIMIT = 6.0e18


def decoder_layer(nc, x, xT, ctxT, wqT, wkT, wvT, woT, lam_in, g_in, xwT, xb, wgT, wuT, wdT, out):
    with ExitStack() as ctx:
        def sb(name, shape, dt=F32):
            return ctx.enter_context(nc.sbuf_tensor(name, shape, dt))

        def sem(name):
            return ctx.enter_context(nc.semaphore(name))

        wq_sb, wk_sb, wv_sb, wo_sb = (sb(n, [P, EB, E]) for n in ("wq_sb", "wk_sb", "wv_sb", "wo_sb"))
        wog = sb("wog", [P, EB, E])
        g_sb = sb("g_sb", [P, EB])
        xw_sb = sb("xw_sb", [P, 2, C])
        xb_sb = sb("xb_sb", [P, 2])
        wg_sb, wu_sb = sb("wg_sb", [P, EB, F]), sb("wu_sb", [P, EB, F])
        wd_sb = sb("wd_sb", [P, FB, E])
        ident = sb("ident", [P, P])
        ident_bf = sb("ident_bf", [P, P], BF16)
        mask = sb("mask", [P, 4, P], BF16)
        zeros = sb("zeros", [N2, T], BF16)
        half_power = sb("half_power", [P, 8])
        lam_sb = sb("lam_sb", [P, 4, D])
        lam_w = sb("lam_w", [P, 2, D])
        lam_d = sb("lam_d", [P, 2])
        lam_e = sb("lam_e", [P, 2])
        neg_lam = sb("neg_lam", [P, 1])
        x_tok = sb("x_tok", [P, TB, E])
        x_tr = sb("x_tr", [P, EB, T])
        ctx_tr = sb("ctx_tr", [P, T])
        qk = sb("qk", [P, 2, 2, T])
        q_part = sb("q_part", [P, PARTS, 2, T], BF16)
        k_part = sb("k_part", [P, PARTS, 2, T], BF16)
        q_rest = sb("q_rest", [P, 2, T])
        k_rest = sb("k_rest", [P, 2, T])
        q_stack = sb("q_stack", [P, N2, T], BF16)
        k_stack = sb("k_stack", [P, N2, T], BF16)
        v_sb = sb("v_sb", [P, TB, H, 32])
        nmax6 = sb("nmax6", [P, H, 6])
        nmax = sb("nmax", [P, TB, N2])
        m_rest = sb("m_rest", [P, TB, N2])
        m_part = sb("m_part", [P, TB, PARTS, N2], BF16)
        mT = sb("mT", [PARTS * N2, T], BF16)
        prob = sb("prob", [P, RING, 768])
        oT = sb("oT", [P, 2, 512])
        rsum = sb("rsum", [P, 2, 8])
        a_map = sb("a_map", [P, 2, 2, 8 * DV])
        o_q = sb("o_q", [P, 2, 2, 4 * DV])
        o_sq = sb("o_sq", [P, 8, DV])
        ss = sb("ss", [P, 2, 8])
        ms = sb("ms", [P, 2, 8])
        rms = sb("rms", [P, 2, 8])
        o_tok = sb("o_tok", [P, TB, E])
        o_tr = sb("o_tr", [P, EB, T])
        qkx = sb("qkx", [P, 2, T])
        neg_emax = sb("neg_emax", [P, TB])
        esum = sb("esum", [P, TB])
        erec = sb("erec", [P, TB])
        e_sb = sb("e_sb", [P, TB, T])
        attn_x = sb("attn_x", [P, TB, T])
        attn_xT = sb("attn_xT", [P, TB, T])
        z = sb("z", [P, TB, E])
        stats = sb("stats", [P, TB, 6])
        mv = sb("mv", [P, TB, 2])
        var_eps = sb("var_eps", [P, TB])
        rstd = sb("rstd", [P, TB])
        x1, x2, x3 = (sb(n, [P, TB, E]) for n in ("x1", "x2", "x3"))
        x1T, x2T = sb("x1T", [P, EB, T]), sb("x2T", [P, EB, T])
        th = sb("th", [P, 2, T])
        gated = sb("gated", [P, 2, T])
        hT = sb("hT", [P, 4, T])

        score = [ctx.enter_context(nc.psum_tensor(f"score{i}", [P, 1024], F32)) for i in range(2)]
        pv_bank = ctx.enter_context(nc.psum_tensor("pv_bank", [P, 512], F32))
        t0, t1, t2 = (ctx.enter_context(nc.psum_tensor(f"t{i}", [P, 512], F32)) for i in range(3))

        names_in = "x_tr x_tok ctx_tr wq wk wv wo lam g xw xb wg wu wd".split()
        loaded = {n: sem(f"in_{n}") for n in names_in}
        stack0_in, stack1_in = sem("stack0_in"), sem("stack1_in")
        m_rows_in = sem("m_rows_in")
        stored = sem("stored")
        pool_const, dve_const, lam_dots, lam_exp = sem("pool_const"), sem("dve_const"), sem("lam_dots"), sem("lam_exp")
        q_proj, k_proj, v_proj = sem("q_proj"), sem("k_proj"), sem("v_proj")
        q_out, k_out, v_out = sem("q_out"), sem("k_out"), sem("v_out")
        q_clamped, q_parts, k_parts = sem("q_clamped"), sem("q_parts"), sem("k_parts")
        s_ready, s_max = sem("s_ready"), sem("s_max")
        m_parts, mT_ready, mT_out = sem("m_parts"), sem("mT_ready"), sem("mT_out")
        st_ready, exp_done, masked = sem("st_ready"), sem("exp_done"), sem("masked")
        pv_ready, pv_out, pvT_ready, pvT_used = sem("pv_ready"), sem("pv_out"), sem("pvT_ready"), sem("pvT_used")
        ss_ready, rms_ready, o_ready = sem("ss_ready"), sem("rms_ready"), sem("o_ready")
        qkx_ready, qkx_out = sem("qkx_ready"), sem("qkx_out")
        oT_ready, oT_out, y_ready = sem("oT_ready"), sem("oT_out"), sem("y_ready")
        e_ready, e_max, e_exp, a_ready = sem("e_ready"), sem("e_max"), sem("e_exp"), sem("a_ready")
        aT_ready, aT_out = sem("aT_ready"), sem("aT_out")
        z1_done, z2_done, z3_done = sem("z1_done"), sem("z2_done"), sem("z3_done")
        var_ready, rstd_ready = sem("var_ready"), sem("rstd_ready")
        x1_done, x2_done, x3_done = sem("x1_done"), sem("x2_done"), sem("x3_done")
        x1T_ready, x1T_out, x2T_ready, x2T_out = sem("x1T_ready"), sem("x1T_out"), sem("x2T_ready"), sem("x2T_out")
        xm_ready = sem("xm_ready")
        hid_ready, tanh_done, h_done, down_ready = sem("hid_ready"), sem("tanh_done"), sem("h_done"), sem("down_ready")
        dve_step, pool_step = sem("dve_step"), sem("pool_step")

        block = ctx.enter_context(nc.Block())

        def wait(eng, s, n):
            if n > 0:
                eng.wait_ge(s, n)

        @block.sync
        def _(sp):
            def load(dst, src, name):
                sp.dma_start(dst, src).then_inc(loaded[name], 16)

            load(x_tr[:], xT[0], "x_tr")
            load(wq_sb[:], wqT, "wq")
            load(wk_sb[:], wkT, "wk")
            load(wv_sb[:], wvT, "wv")
            load(x_tok[:], x[0], "x_tok")
            load(lam_sb[:], lam_in, "lam")
            load(ctx_tr[:], ctxT[0], "ctx_tr")

            def stack_half(half, s):
                hs = slice(HALF * half, HALF * half + HALF)
                for g, (pq, pk) in enumerate(PAIRS):
                    rows = slice(D * g, D * g + D)
                    for stack, part, p in ((q_stack, q_part, pq), (k_stack, k_part, pk)):
                        sp.dma_start(stack[rows, hs, :], part[:, p, half, :]).then_inc(s, 16)

            def body(b):
                sp.wait_ge(q_parts, b + 1)
                sp.wait_ge(k_parts, b + 1)
                if b == 0:
                    sp.wait_ge(pool_const, 7)
                    sp.wait_ge(dve_const, 4)
                for p in range(PARTS):
                    sp.dma_start(q_stack[M_ROW + p:M_ROW + p + 1, :, :], zeros[:]).then_inc(stack0_in, 16)
                stack_half(0, stack0_in)
                stack_half(1, stack1_in)
                if b + 1 < B:
                    sp.wait_ge(v_proj, b + 1)
                    load(x_tr[:], xT[b + 1], "x_tr")
                if b > 0:
                    sp.wait_ge(qkx_ready, b)
                    load(ctx_tr[:], ctxT[b], "ctx_tr")
                    sp.wait_ge(z1_done, b)
                    load(x_tok[:], x[b], "x_tok")
                sp.wait_ge(mT_out, b + 1)
                for p in range(PARTS):
                    sp.dma_start(q_stack[M_ROW + p:M_ROW + p + 1, :, :],
                                 mT[N2 * p:N2 * p + N2, :]).then_inc(m_rows_in, 16)
                if b > 0:
                    store(b - 1)

            def store(t):
                sp.wait_ge(x3_done, t + 1)
                sp.dma_start(out[t], x3[:]).then_inc(stored, 16)

            for b in range(B):
                body(b)
            store(B - 1)
            sp.wait_ge(stored, 16 * B)

        @block.gpsimd
        def _(pool):
            step = [0]

            def link(ins):
                step[0] += 1
                ins.then_inc(pool_step, 1)
                pool.wait_ge(pool_step, step[0])

            nc.gpsimd.memset(ident[:], 0.0).then_inc(pool_const, 1)
            nc.gpsimd.memset(mask[:], 0.0).then_inc(pool_const, 1)
            nc.gpsimd.memset(half_power[:], -0.5).then_inc(pool_const, 1)
            pool.wait_ge(pool_const, 3)
            nc.gpsimd.affine_select(out=ident[:], in_=ident[:], compare_op=ALU.not_equal, fill=1.0, base=0,
                                    pattern=[[-1, P]], channel_multiplier=1).then_inc(pool_const, 1)
            nc.gpsimd.affine_select(out=mask[:], in_=mask[:], compare_op=ALU.is_ge, fill=MASKED, base=0,
                                    pattern=[[0, 4], [-1, P]], channel_multiplier=1).then_inc(pool_const, 1)
            nc.gpsimd.memset(k_stack[:].bitcast(U32), 0).then_inc(pool_const, 1)
            nc.gpsimd.memset(zeros[:], 0.0).then_inc(pool_const, 1)

            def q_split(b):
                pool.wait_ge(q_clamped, b + 1)
                wait(pool, stack1_in, 12 * 16 * b)
                wait(pool, stack0_in, 15 * 16 * b)
                q = qk[:, 0]
                link(nc.gpsimd.tensor_scalar(q_part[:, 0], q, 1.0, 0.0, ALU.mult, ALU.add))
                link(nc.gpsimd.tensor_tensor(q_rest[:], q, q_part[:, 0], ALU.subtract))
                link(nc.gpsimd.tensor_scalar(q_part[:, 1], q_rest[:], 1.0, 0.0, ALU.mult, ALU.add))
                link(nc.gpsimd.tensor_tensor(q_rest[:], q_rest[:], q_part[:, 1], ALU.subtract))
                nc.gpsimd.tensor_scalar(q_part[:, 2], q_rest[:], 1.0, 0.0, ALU.mult, ALU.add).then_inc(q_parts, 1)

            def layer_rstd(t, n):
                pool.wait_ge(var_ready, 3 * t + n + 1)
                link(nc.gpsimd.tensor_scalar(var_eps[:], mv[:, :, 1], 1.0, EPS, ALU.mult, ALU.add))
                nc.gpsimd.tensor_tensor(rstd[:], var_eps[:], half_power[:, 0:TB], ALU.pow).then_inc(rstd_ready, 1)

            def causal(b, u):
                pool.wait_ge(exp_done, H * b + u + 1)
                p = prob[:, u % RING, :]
                first = p[:, 0:512].rearrange("p (c q) -> p c q", c=2)[:, :, 0:P]
                nc.gpsimd.affine_select(out=first, in_=first, compare_op=ALU.is_ge, fill=0.0, base=0,
                                        pattern=[[0, 2], [1, P]], channel_multiplier=-1)
                second = p[:, 512:768].rearrange("p (c q) -> p c q", c=2)
                nc.gpsimd.affine_select(out=second, in_=second, compare_op=ALU.is_ge, fill=0.0, base=0,
                                        pattern=[[0, 2], [1, P]], channel_multiplier=-1).then_inc(masked, 1)

            def head_rms(b, quad):
                pool.wait_ge(ss_ready, QUADS * b + quad + 1)
                s = quad % 2
                link(nc.gpsimd.tensor_scalar(ms[:, s], ss[:, s], 1.0 / DV, EPS, ALU.mult, ALU.add))
                nc.gpsimd.tensor_tensor(rms[:, s], ms[:, s], half_power[:], ALU.pow).then_inc(rms_ready, 1)

            def body(b, tail):
                q_split(b)
                if tail:
                    for n in range(3):
                        layer_rstd(b - 1, n)
                for u in range(H):
                    causal(b, u)
                    if u % 4 == 3 and u > 3:
                        head_rms(b, u // 4 - 1)
                head_rms(b, QUADS - 1)

            body(0, False)
            for b in range(1, B):
                body(b, True)
            for n in range(3):
                layer_rstd(B - 1, n)

        @block.scalar
        def _(act):
            def load(dst, src, name):
                act.dma_start(dst, src).then_inc(loaded[name], 16)

            load(wo_sb[:], woT, "wo")
            load(g_sb[:], g_in, "g")
            load(xw_sb[:], xwT, "xw")
            load(xb_sb[:], xb, "xb")
            load(wg_sb[:], wgT, "wg")
            load(wu_sb[:], wuT, "wu")
            load(wd_sb[:], wdT, "wd")
            act.wait_ge(lam_dots, 1)
            nc.scalar.activation(lam_e[:], lam_d[:], ACT.Exp).then_inc(lam_exp, 1)

            def flat(t):
                return t.rearrange("p a b -> p (a b)")

            def qkv_out(b):
                act.wait_ge(q_proj, b + 1)
                wait(act, q_parts, b)
                wait(act, k_parts, b)
                nc.scalar.activation(flat(qk[:, 0]), t0[:], ACT.Copy, scale=SCALING).then_inc(q_out, 1)
                act.wait_ge(k_proj, b + 1)
                nc.scalar.activation(flat(qk[:, 1]), t1[:], ACT.Copy).then_inc(k_out, 1)
                act.wait_ge(v_proj, b + 1)
                wait(act, pv_ready, QUADS * b)
                if b == 0:
                    act.wait_ge(dve_const, 4)
                nc.scalar.activation(v_sb[:, :, :, 0:DV], t2[:].rearrange("p (a h d) -> p a h d", a=TB, h=H),
                                     ACT.Copy).then_inc(v_out, 1)

            def tail_start(t):
                act.wait_ge(qkx_ready, t + 1)
                if t == 0:
                    act.wait_ge(loaded["xb"], 16)
                for i in range(2):
                    nc.scalar.activation(qkx[:, i], t0[:, T * i:T * i + T], ACT.Identity,
                                         bias=xb_sb[:, i:i + 1]).then_inc(qkx_out, 1)
                act.wait_ge(oT_ready, t + 1)
                nc.scalar.activation(flat(o_tr[:]), t1[:], ACT.Copy).then_inc(oT_out, 1)
                act.wait_ge(e_max, t + 1)
                for i in range(TB):
                    nc.scalar.activation(e_sb[:, i], t2[:, T * i:T * i + T], ACT.Exp, bias=neg_emax[:, i:i + 1],
                                         accum_out=esum[:, i:i + 1]).then_inc(e_exp, 1)
                act.wait_ge(aT_ready, t + 1)
                nc.scalar.activation(flat(attn_xT[:]), t1[:], ACT.Copy).then_inc(aT_out, 1)

            def tail_middle(t):
                act.wait_ge(x1T_ready, t + 1)
                nc.scalar.activation(flat(x1T[:]), t2[:], ACT.Copy).then_inc(x1T_out, 1)
                act.wait_ge(x2T_ready, t + 1)
                nc.scalar.activation(flat(x2T[:]), t1[:], ACT.Copy).then_inc(x2T_out, 1)

            def tanh_gate(t, j):
                act.wait_ge(hid_ready, FB * t + j + 1)
                wait(act, h_done, FB * t + j - 1)
                nc.scalar.activation(th[:, j % 2], (t0, t2)[j % 2][:, 0:T], ACT.Tanh, scale=0.5).then_inc(tanh_done, 1)

            def m_out(b):
                act.wait_ge(mT_ready, b + 1)
                wait(act, m_rows_in, 48 * b)
                nc.scalar.activation(mT[:], pv_bank[0:PARTS * N2, 0:T // 2].bitcast(BF16), ACT.Copy).then_inc(mT_out, 1)

            def probs(b):
                for u in range(H + 2):
                    if u < H:
                        act.wait_ge(st_ready, H * b + u + 1)
                        wait(act, pv_ready, QUADS * b + u // 4 - 1)
                        nc.scalar.activation(prob[:, u % RING, :], score[u % 2][:, 0:768], ACT.Exp).then_inc(exp_done, 1)
                    if u >= 5 and (u - 5) % 4 == 0:
                        quad = (u - 5) // 4
                        act.wait_ge(pv_ready, QUADS * b + quad + 1)
                        wait(act, pvT_ready, QUADS * b + quad - 1)
                        nc.scalar.activation(oT[:, quad % 2], pv_bank[:], ACT.Copy).then_inc(pv_out, 1)

            def body(b, tail):
                qkv_out(b)
                if tail:
                    tail_start(b - 1)
                    tail_middle(b - 1)
                    for j in range(FB - 1):
                        tanh_gate(b - 1, j)
                m_out(b)
                if tail:
                    tanh_gate(b - 1, FB - 1)
                probs(b)

            body(0, False)
            for b in range(1, B):
                body(b, True)
            tail_start(B - 1)
            tail_middle(B - 1)
            for j in range(FB):
                tanh_gate(B - 1, j)

        @block.tensor
        def _(pe):
            def matmuls(out_ap, pairs):
                for n, (lhsT, rhs) in enumerate(pairs):
                    mm = nc.tensor.matmul(out_ap, lhsT, rhs, start=(n == 0), stop=(n == len(pairs) - 1))
                return mm

            def blk(i):
                return slice(P * i, P * i + P)

            def project_qkv(b):
                pe.wait_ge(loaded["x_tr"], 16 * (b + 1))
                for t, w, name, done in ((t0, wq_sb, "wq", q_proj), (t1, wk_sb, "wk", k_proj)):
                    if b == 0:
                        pe.wait_ge(loaded[name], 16)
                    elif t is t0:
                        pe.wait_ge(pvT_used, QUADS * b - 1)
                    else:
                        wait(pe, z3_done, b - 1)
                    for half in range(2):
                        mm = matmuls(t[:, T * half:T * half + T],
                                     [(w[:, e, blk(half)], x_tr[:, e, :]) for e in range(EB)])
                    mm.then_inc(done, 1)
                if b == 0:
                    pe.wait_ge(loaded["wv"], 16)
                wait(pe, pvT_used, QUADS * b)
                for i in range(TB):
                    mm = matmuls(t2[:, E * i:E * i + E], [(x_tr[:, e, blk(i)], wv_sb[:, e, :]) for e in range(EB)])
                mm.then_inc(v_proj, 1)

            def four_transposes(bank, src):
                for i in range(2):
                    for j in range(2):
                        mm = nc.tensor.transpose(bank[:, T * j + P * i:T * j + P * i + P], src[:, i, blk(j)], ident[:])
                return mm

            def tail_start(t, b):
                pe.wait_ge(loaded["ctx_tr"], 16 * (t + 1))
                if t == 0:
                    pe.wait_ge(loaded["xw"], 16)
                pe.wait_ge(q_out, b + 1) if b < B else pe.wait_ge(pvT_used, QUADS * b - 1)
                for i in range(2):
                    mm = nc.tensor.matmul(t0[:, T * i:T * i + T], xw_sb[:, i, :], ctx_tr[:], start=True, stop=True)
                mm.then_inc(qkx_ready, 1)
                pe.wait_ge(o_ready, QUADS * (t + 1))
                pe.wait_ge(k_out, b + 1) if b < B else pe.wait_ge(z3_done, b - 1)
                four_transposes(t1, o_tok).then_inc(oT_ready, 1)
                pe.wait_ge(qkx_out, 2 * (t + 1))
                pe.wait_ge(v_out, b + 1) if b < B else pe.wait_ge(pvT_used, QUADS * b)
                for i in range(TB):
                    mm = nc.tensor.matmul(t2[:, T * i:T * i + T], qkx[:, 0, blk(i)], qkx[:, 1, :], start=True, stop=True)
                mm.then_inc(e_ready, 1)
                pe.wait_ge(oT_out, t + 1)
                if t == 0:
                    pe.wait_ge(dve_const, 6)
                for i in range(TB):
                    mm = matmuls(t0[:, E * i:E * i + E], [(o_tr[:, e, blk(i)], wog[:, e, :]) for e in range(EB)])
                mm.then_inc(y_ready, 1)
                pe.wait_ge(a_ready, t + 1)
                four_transposes(t1, attn_x).then_inc(aT_ready, 1)

            def x1_transposed(t):
                pe.wait_ge(x1_done, t + 1)
                pe.wait_ge(e_exp, 2 * (t + 1))
                four_transposes(t2, x1).then_inc(x1T_ready, 1)

            def cross(t):
                pe.wait_ge(x1T_out, t + 1)
                pe.wait_ge(aT_out, t + 1)
                pe.wait_ge(z1_done, t + 1)
                for i in range(TB):
                    mm = matmuls(t0[:, T * i:T * i + T], [(x1T[:, n, blk(i)], attn_xT[:, n, :]) for n in range(TB)])
                mm.then_inc(xm_ready, 1)

            def x2_transposed(t):
                pe.wait_ge(x2_done, t + 1)
                four_transposes(t1, x2).then_inc(x2T_ready, 1)

            def hidden(t, j):
                if j == 0:
                    pe.wait_ge(x2T_out, t + 1)
                    if t == 0:
                        pe.wait_ge(loaded["wg"], 16)
                        pe.wait_ge(loaded["wu"], 16)
                if j >= 2:
                    pe.wait_ge(h_done, FB * t + j - 1)
                bank = (t0, t2)[j % 2]
                for n, w in enumerate((wg_sb, wu_sb)):
                    mm = matmuls(bank[:, T * n:T * n + T], [(w[:, e, blk(j)], x2T[:, e, :]) for e in range(EB)])
                mm.then_inc(hid_ready, 1)

            def down(t, j):
                pe.wait_ge(h_done, FB * t + j + 1)
                if t == 0 and j == 0:
                    pe.wait_ge(loaded["wd"], 16)
                for i in range(TB):
                    mm = nc.tensor.matmul(t1[:, E * i:E * i + E], hT[:, j % 4, blk(i)], wd_sb[:, j, :],
                                          start=(j == 0 and i == 0), stop=(j == FB - 1), skip_group_check=True)
                if j == FB - 1:
                    mm.then_inc(down_ready, 1)

            def scores(b, u):
                if u % 8 == 0:
                    if u == 0:
                        pe.wait_ge(stack0_in, 15 * 16 * (b + 1))
                    else:
                        pe.wait_ge(stack1_in, 12 * 16 * (b + 1))
                if b == 0 and u == 0:
                    pe.wait_ge(pool_const, 7)
                    pe.wait_ge(dve_const, 4)
                if u < 2:
                    wait(pe, exp_done, H * b - 1 + u)
                else:
                    pe.wait_ge(s_max, H * b + u - 1)
                s = score[u % 2]
                first = True
                for m in range(2):
                    n = 2 * u + m
                    for q, k, col in ((0, 0, P * m), (1, 1, 256 + P * m), (1, 0, 512 + P * m)):
                        nc.tensor.matmul(s[:, col:col + P], q_stack[:, n, blk(q)], k_stack[:, n, blk(k)],
                                         start=(first or (col == 512)), stop=(col >= 512), skip_group_check=True)
                        first = False
                nc.tensor.matmul(s[:, 0:512], ident_bf[:], mask[:].rearrange("p a b -> p (a b)"),
                                 start=False, stop=True, skip_group_check=True).then_inc(s_ready, 1)

            def maxima_transposed(b):
                pe.wait_ge(m_parts, b + 1)
                wait(pe, pv_out, QUADS * b)
                for i in range(TB):
                    mm = nc.tensor.transpose(pv_bank[0:PARTS * N2, 64 * i:64 * i + 64].bitcast(BF16),
                                             m_part[:, i].rearrange("p a b -> p (a b)"), ident_bf[:])
                mm.then_inc(mT_ready, 1)

            def scores_transposed(b, u):
                if u == 0:
                    pe.wait_ge(m_rows_in, 48 * (b + 1))
                if u < 2:
                    pe.wait_ge(s_max, H * b + 15 + u)
                else:
                    pe.wait_ge(exp_done, H * b + u - 1)
                s = score[u % 2]
                for m in range(2):
                    n = 2 * u + m
                    nc.tensor.matmul(s[:, T * m:T * m + T], k_stack[:, n, blk(0)], q_stack[:, n, :],
                                     start=True, stop=True)
                for m in range(2):
                    n = 2 * u + m
                    mm = nc.tensor.matmul(s[:, 512 + P * m:512 + P * m + P], k_stack[:, n, blk(1)],
                                          q_stack[:, n, blk(1)], start=True, stop=True)
                mm.then_inc(st_ready, 1)

            def times_v(b, quad):
                pe.wait_ge(masked, H * b + 4 * quad + 4)
                if quad == 0:
                    pe.wait_ge(v_out, b + 1)
                    pe.wait_ge(mT_out, b + 1)
                wait(pe, pv_out, QUADS * b + quad)
                for i in range(4):
                    h = 4 * quad + i
                    nc.tensor.matmul(pv_bank[32 * i:32 * i + 32, :], v_sb[:, 0, h, :], prob[:, h % RING, 0:512],
                                     start=True, stop=False)
                for i in range(4):
                    h = 4 * quad + i
                    late = pv_bank[32 * i:32 * i + 32, :].rearrange("p (m q) -> p m q", m=2)[:, :, P:T]
                    mm = nc.tensor.matmul(late, v_sb[:, 1, h, :], prob[:, h % RING, 512:768].rearrange("p (m q) -> p m q", m=2),
                                          start=False, stop=True)
                mm.then_inc(pv_ready, 1)

            def pv_transposed(b, quad):
                pe.wait_ge(pv_out, QUADS * b + quad + 1)
                if quad >= 2:
                    pe.wait_ge(pvT_used, QUADS * b + quad - 1)
                else:
                    wait(pe, h_done, FB * b)
                bank = (t0, t2)[quad % 2]
                for i in range(4):
                    mm = nc.tensor.transpose(bank[:, blk(i)], oT[:, quad % 2, blk(i)], ident[:])
                mm.then_inc(pvT_ready, 1)

            def body(b, tail):
                t = b - 1
                project_qkv(b)
                if tail:
                    tail_start(t, b)
                scores(b, 0)
                scores(b, 1)
                if tail:
                    x1_transposed(t)
                scores(b, 2)
                scores(b, 3)
                if tail:
                    cross(t)
                scores(b, 4)
                scores(b, 5)
                if tail:
                    x2_transposed(t)
                for j in range(5):
                    if tail:
                        hidden(t, j)
                    scores(b, 6 + 2 * j)
                    scores(b, 7 + 2 * j)
                    if tail and j > 0:
                        down(t, j - 1)
                if tail:
                    hidden(t, 5)
                    down(t, 4)
                    hidden(t, 6)
                    down(t, 5)
                maxima_transposed(b)
                if tail:
                    hidden(t, 7)
                    down(t, 6)
                    down(t, 7)
                for u in range(H + 2):
                    if u < H:
                        scores_transposed(b, u)
                    if u >= 5 and (u - 5) % 4 == 0:
                        times_v(b, (u - 5) // 4)
                    if u >= 7 and (u - 7) % 4 == 0:
                        pv_transposed(b, (u - 7) // 4)
                pv_transposed(b, QUADS - 1)

            body(0, False)
            for b in range(1, B):
                body(b, True)
            t = B - 1
            tail_start(t, B)
            x1_transposed(t)
            cross(t)
            x2_transposed(t)
            for j in range(FB):
                hidden(t, j)
                if j > 0:
                    down(t, j - 1)
            down(t, FB - 1)

        @block.vector
        def _(dve):
            step = [0]

            def link(ins):
                step[0] += 1
                ins.then_inc(dve_step, 1)
                dve.wait_ge(dve_step, step[0])

            nc.vector.memset(q_stack[:].bitcast(U32), 0).then_inc(dve_const, 1)
            link(nc.vector.memset(v_sb[:], 0.0))
            nc.vector.memset(v_sb[:, :, :, DV:DV + 1], 1.0).then_inc(dve_const, 1)
            dve.wait_ge(pool_const, 4)
            nc.vector.tensor_copy(ident_bf[:], ident[:]).then_inc(dve_const, 1)
            dve.wait_ge(pool_const, 6)
            nc.vector.memset(k_stack[32:64, :, :].bitcast(U32), 0x3F803F80).then_inc(dve_const, 1)
            dve.wait_ge(loaded["lam"], 16)
            nc.vector.tensor_tensor_reduce(lam_w[:, 0], lam_sb[:, 0], lam_sb[:, 1], 1.0, 0.0, ALU.mult, ALU.add,
                                           lam_d[:, 0:1])
            nc.vector.tensor_tensor_reduce(lam_w[:, 1], lam_sb[:, 2], lam_sb[:, 3], 1.0, 0.0, ALU.mult, ALU.add,
                                           lam_d[:, 1:2]).then_inc(lam_dots, 1)

            def split_k(b):
                dve.wait_ge(q_out, b + 1)
                nc.vector.tensor_scalar(qk[:, 0], qk[:, 0], -LIMIT, LIMIT, ALU.max, ALU.min).then_inc(q_clamped, 1)
                dve.wait_ge(k_out, b + 1)
                k = qk[:, 1]
                link(nc.vector.tensor_scalar(k, k, -LIMIT, LIMIT, ALU.max, ALU.min))
                wait(dve, stack0_in, 15 * 16 * b)
                wait(dve, stack1_in, 12 * 16 * b)
                link(nc.vector.tensor_copy(k_part[:, 0], k))
                link(nc.vector.tensor_tensor(k_rest[:], k, k_part[:, 0], ALU.subtract))
                link(nc.vector.tensor_copy(k_part[:, 1], k_rest[:]))
                link(nc.vector.tensor_tensor(k_rest[:], k_rest[:], k_part[:, 1], ALU.subtract))
                nc.vector.tensor_copy(k_part[:, 2], k_rest[:]).then_inc(k_parts, 1)

            def score_max(b, u):
                dve.wait_ge(s_ready, H * b + u + 1)
                nc.vector.tensor_reduce(nmax6[:, u, :], score[u % 2][:, 0:768].rearrange("p (a k) -> p a k", k=P),
                                        AX.X, ALU.max, negate=True).then_inc(s_max, 1)

            def split_maxima(b):
                dve.wait_ge(s_max, H * (b + 1))
                wait(dve, mT_ready, b)
                nc.vector.tensor_copy(nmax[:, 0, :].rearrange("p (h m) -> p h m", m=2), nmax6[:, :, 0:2])
                link(nc.vector.tensor_tensor(nmax[:, 1, :].rearrange("p (h m) -> p h m", m=2), nmax6[:, :, 2:4],
                                             nmax6[:, :, 4:6], ALU.min))
                link(nc.vector.tensor_copy(m_part[:, :, 0], nmax[:]))
                link(nc.vector.tensor_tensor(m_rest[:], nmax[:], m_part[:, :, 0], ALU.subtract))
                link(nc.vector.tensor_copy(m_part[:, :, 1], m_rest[:]))
                link(nc.vector.tensor_tensor(m_rest[:], m_rest[:], m_part[:, :, 1], ALU.subtract))
                nc.vector.tensor_copy(m_part[:, :, 2], m_rest[:]).then_inc(m_parts, 1)

            def combine(b, quad):
                s = quad % 2
                dve.wait_ge(pvT_ready, QUADS * b + quad + 1)
                bank = (t0, t2)[s]
                maps = bank[:].rearrange("p (m r c) -> p m r c", m=2, c=32)
                rs = rsum[:, 0:2, :]
                link(nc.vector.reciprocal(rs, maps[:, :, :, DV]))
                for m in range(2):
                    ins = nc.vector.tensor_tensor(a_map[:, s, m].rearrange("p (r c) -> p r c", c=DV), maps[:, m, :, 0:DV],
                                                  rsum[:, m, :].unsqueeze(2).to_broadcast([P, 8, DV]), ALU.mult)
                ins.then_inc(pvT_used, 1)
                dve.wait_ge(pvT_used, QUADS * b + quad + 1)
                o = o_q[:, s].rearrange("p a b -> p (a b)")
                link(nc.vector.scalar_tensor_tensor(out=o, in0=a_map[:, s, 1], scalar=neg_lam[:, 0:1],
                                                    in1=a_map[:, s, 0], op0=ALU.mult, op1=ALU.add))
                link(nc.vector.tensor_tensor(o_sq[:].rearrange("p r c -> p (r c)"), o, o, ALU.mult))
                nc.vector.tensor_reduce(ss[:, s], o_sq[:], AX.X, ALU.add).then_inc(ss_ready, 1)

            def normalise(b, quad):
                s = quad % 2
                dve.wait_ge(rms_ready, QUADS * b + quad + 1)
                wait(dve, oT_ready, b)
                for i in range(TB):
                    ins = nc.vector.tensor_tensor(
                        o_tok[:, i, 4 * DV * quad:4 * DV * (quad + 1)].rearrange("p (h c) -> p h c", c=DV),
                        o_q[:, s, i].rearrange("p (h c) -> p h c", c=DV),
                        rms[:, s, 4 * i:4 * i + 4].unsqueeze(2).to_broadcast([P, 4, DV]), ALU.mult)
                ins.then_inc(o_ready, 1)

            def layer_stats():
                for i in range(TB):
                    ins = nc.vector.bn_stats(stats[:, i], z[:, i])
                link(ins)
                for i in range(TB):
                    ins = nc.vector.bn_aggr(mv[:, i], stats[:, i])
                ins.then_inc(var_ready, 1)

            def layer_norm(t, n, dst, done):
                dve.wait_ge(rstd_ready, 3 * t + n + 1)
                for i in range(TB):
                    ins = nc.vector.tensor_scalar(dst[:, i], z[:, i], mv[:, i, 0:1], rstd[:, i:i + 1],
                                                  ALU.subtract, ALU.mult)
                ins.then_inc(done, 1)

            def flat(t):
                return t.rearrange("p a b -> p (a b)")

            def tail_start(t):
                dve.wait_ge(e_ready, t + 1)
                nc.vector.tensor_reduce(neg_emax[:], t2[:].rearrange("p (a k) -> p a k", a=TB), AX.X, ALU.max,
                                        negate=True).then_inc(e_max, 1)
                dve.wait_ge(e_exp, 2 * (t + 1))
                link(nc.vector.reciprocal(erec[:], esum[:]))
                for i in range(TB):
                    ins = nc.vector.tensor_scalar(attn_x[:, i], e_sb[:, i], erec[:, i:i + 1], None, ALU.mult)
                ins.then_inc(a_ready, 1)
                dve.wait_ge(y_ready, t + 1)
                dve.wait_ge(loaded["x_tok"], 16 * (t + 1))
                nc.vector.tensor_tensor(flat(z[:]), t0[:], flat(x_tok[:]), ALU.add).then_inc(z1_done, 1)
                dve.wait_ge(z1_done, t + 1)
                layer_stats()

            def second_residual(t):
                dve.wait_ge(xm_ready, t + 1)
                nc.vector.tensor_tensor(flat(z[:]), t0[:], flat(x1[:]), ALU.add).then_inc(z2_done, 1)
                dve.wait_ge(z2_done, t + 1)
                layer_stats()

            def gate(t, j):
                dve.wait_ge(tanh_done, FB * t + j + 1)
                bank = (t0, t2)[j % 2]
                link(nc.vector.scalar_tensor_tensor(out=gated[:, j % 2], in0=th[:, j % 2], scalar=1.0,
                                                    in1=bank[:, 0:T], op0=ALU.add, op1=ALU.mult))
                nc.vector.tensor_tensor(hT[:, j % 4], gated[:, j % 2], bank[:, T:2 * T], ALU.mult).then_inc(h_done, 1)

            def third_residual(t):
                dve.wait_ge(down_ready, t + 1)
                nc.vector.scalar_tensor_tensor(out=flat(z[:]), in0=t1[:], scalar=0.5, in1=flat(x2[:]), op0=ALU.mult,
                                               op1=ALU.add).then_inc(z3_done, 1)
                dve.wait_ge(z3_done, t + 1)
                layer_stats()
                wait(dve, stored, 16 * t)
                layer_norm(t, 2, x3, x3_done)

            def late_constants():
                dve.wait_ge(lam_exp, 1)
                link(nc.vector.scalar_tensor_tensor(out=neg_lam[:], in0=lam_e[:, 1:2], scalar=LAMBDA_INIT,
                                                    in1=lam_e[:, 0:1], op0=ALU.subtract, op1=ALU.subtract))
                dve.wait_ge(loaded["wo"], 16)
                dve.wait_ge(loaded["g"], 16)
                for e in range(EB):
                    nc.vector.tensor_scalar(wog[:, e], wo_sb[:, e], g_sb[:, e:e + 1], 1.0 - LAMBDA_INIT,
                                            ALU.mult, ALU.mult).then_inc(dve_const, 1)

            def body(b, tail):
                t = b - 1
                split_k(b)
                if b == 0:
                    late_constants()
                if tail:
                    tail_start(t)
                score_max(b, 0)
                if tail:
                    layer_norm(t, 0, x1, x1_done)
                score_max(b, 1)
                score_max(b, 2)
                score_max(b, 3)
                if tail:
                    second_residual(t)
                score_max(b, 4)
                if tail:
                    layer_norm(t, 1, x2, x2_done)
                score_max(b, 5)
                for j in range(5):
                    if tail:
                        gate(t, j)
                    score_max(b, 6 + 2 * j)
                    score_max(b, 7 + 2 * j)
                split_maxima(b)
                if tail:
                    for j in range(5, FB):
                        gate(t, j)
                    third_residual(t)
                for quad in range(QUADS):
                    combine(b, quad)
                    if quad > 0:
                        normalise(b, quad - 1)
                normalise(b, QUADS - 1)

            body(0, False)
            for b in range(1, B):
                body(b, True)
            t = B - 1
            tail_start(t)
            layer_norm(t, 0, x1, x1_done)
            second_residual(t)
            layer_norm(t, 1, x2, x2_done)
            for j in range(FB):
                gate(t, j)
            third_residual(t)


def kernel(x, ctx_1024, L0_attn_Wq, L0_attn_Wk, L0_attn_Wv, L0_attn_Wo, L0_attn_lambda_q1, L0_attn_lambda_k1,
           L0_attn_lambda_q2, L0_attn_lambda_k2, L0_attn_subln_weight, L0_xattn_Wq, L0_xattn_bq, L0_xattn_Wk,
           L0_xattn_bk, L0_ffn_w_gate, L0_ffn_w_up, L0_ffn_w_down):
    import concourse.bacc as bacc
    import numpy as np
    from concourse.bass_utils import run_bass_kernel_spmd

    def rows(a, n):
        a = np.asarray(a)
        return np.ascontiguousarray(a.reshape(n, P, -1).transpose(1, 0, 2))

    def half_heads(w):
        return np.asarray(w).reshape(2, HALF, D, E).transpose(0, 2, 1, 3).reshape(E, E)

    x = np.asarray(x)
    context = np.asarray(ctx_1024)
    arrays = {
        "x": np.stack([rows(x[b], TB) for b in range(B)]),
        "xT": np.stack([rows(x[b].T, EB) for b in range(B)]),
        "ctxT": np.ascontiguousarray(context.transpose(0, 2, 1)),
        "wqT": rows(half_heads(L0_attn_Wq).T, EB),
        "wkT": rows(half_heads(L0_attn_Wk).T, EB),
        "wvT": rows(np.asarray(L0_attn_Wv).T, EB),
        "woT": rows(np.asarray(L0_attn_Wo).T, EB),
        "lam_in": np.ascontiguousarray(np.broadcast_to(np.stack([
            np.asarray(a) for a in (L0_attn_lambda_q1, L0_attn_lambda_k1, L0_attn_lambda_q2, L0_attn_lambda_k2)]),
            (P, 4, D))),
        "g_in": np.ascontiguousarray(np.tile(np.asarray(L0_attn_subln_weight), H).reshape(EB, P).T),
        "xwT": np.ascontiguousarray(np.stack([np.asarray(L0_xattn_Wq).T, np.asarray(L0_xattn_Wk).T], 1)),
        "xb": np.ascontiguousarray(np.stack([np.asarray(L0_xattn_bq), np.asarray(L0_xattn_bk)], 1)),
        "wgT": rows(np.asarray(L0_ffn_w_gate).T, EB),
        "wuT": rows(np.asarray(L0_ffn_w_up).T, EB),
        "wdT": rows(np.asarray(L0_ffn_w_down).T, FB),
    }
    nc = bacc.Bacc("TRN2", target_bir_lowering=False, num_devices=1)
    ins = [nc.dram_tensor(n, a.shape, mybir.dt.from_np(a.dtype), kind="ExternalInput").ap() for n, a in arrays.items()]
    out = nc.dram_tensor("out", (B, P, TB, E), F32, kind="ExternalOutput").ap()
    decoder_layer(nc, *ins, out)
    got = run_bass_kernel_spmd(nc, [arrays], core_ids=[0]).results[0]["out"]
    return np.ascontiguousarray(got.transpose(0, 2, 1, 3)).reshape(B, T, E)
```

```python
import math
from contextlib import ExitStack

import concourse.bass as bass
from concourse import mybir
from concourse.alu_op_type import AluOpType as ALU

ACT = mybir.ActivationFunctionType
AX = mybir.AxisListType
F32 = mybir.dt.float32
BF16 = mybir.dt.bfloat16
U32 = mybir.dt.uint32

P = 128
B, T, E = 4, 256, 256
TB, EB = T // P, E // P
H = 16
N2 = 2 * H
D = E // N2
DV = 2 * D
C = 128
F = 1024
FB = F // P
PARTS = 3
PAIRS = ((0, 0), (0, 1), (1, 0), (1, 1), (0, 2), (2, 0))
M_ROW = D * len(PAIRS)
QUADS = H // 4
RING = 8
LAMBDA_INIT = 0.8 - 0.6 * math.exp(-0.3 * 12)
SCALING = D ** -0.5
EPS = 1e-5
MASKED = -3.0e38
LIMIT = 6.0e18


def decoder_layer(nc, x, xT, ctxT, wqT, wkT, wvT, woT, lam_in, g_in, xwT, xb, wgT, wuT, wdT, out):
    with ExitStack() as ctx:
        def sb(name, shape, dt=F32):
            return ctx.enter_context(nc.sbuf_tensor(name, shape, dt))

        def sem(name):
            return ctx.enter_context(nc.semaphore(name))

        wq_sb, wk_sb, wv_sb, wo_sb = (sb(n, [P, EB, E]) for n in ("wq_sb", "wk_sb", "wv_sb", "wo_sb"))
        wog = sb("wog", [P, EB, E])
        g_sb = sb("g_sb", [P, EB])
        xw_sb = sb("xw_sb", [P, 2, C])
        xb_sb = sb("xb_sb", [P, 2])
        wg_sb, wu_sb = sb("wg_sb", [P, EB, F]), sb("wu_sb", [P, EB, F])
        wd_sb = sb("wd_sb", [P, FB, E])
        ident = sb("ident", [P, P])
        ident_bf = sb("ident_bf", [P, P], BF16)
        mask = sb("mask", [P, 4, P], BF16)
        zeros = sb("zeros", [PARTS * N2, T], BF16)
        half_power = sb("half_power", [P, 8])
        lam_sb = sb("lam_sb", [P, 4, D])
        lam_w = sb("lam_w", [P, 2, D])
        lam_d = sb("lam_d", [P, 2])
        lam_e = sb("lam_e", [P, 2])
        neg_lam = sb("neg_lam", [P, 1])
        x_tok = sb("x_tok", [P, TB, E])
        x_tr = sb("x_tr", [P, 2, EB, T])
        ctx_tr = sb("ctx_tr", [P, T])
        qk = sb("qk", [P, 2, 2, T])
        q_part = sb("q_part", [P, 2, PARTS, 2, T], BF16)
        k_part = sb("k_part", [P, 2, PARTS, 2, T], BF16)
        q_stacks = [sb(f"q_stack{i}", [P, N2, T], BF16) for i in range(2)]
        k_stacks = [sb(f"k_stack{i}", [P, N2, T], BF16) for i in range(2)]
        v_sb = sb("v_sb", [P, 3, TB, H, 32])
        nmax6 = sb("nmax6", [P, H, 6])
        nmax = sb("nmax", [P, TB, N2])
        m_rest = sb("m_rest", [P, TB, N2])
        m_part = sb("m_part", [P, TB, PARTS, N2], BF16)
        mT = sb("mT", [PARTS * N2, T], BF16)
        prob = sb("prob", [P, RING, 768])
        oT = sb("oT", [P, 2, 512])
        rsum = sb("rsum", [P, 2, 8])
        a_map = sb("a_map", [P, 2, 2, 8 * DV])
        o_q = sb("o_q", [P, 2, 2, 4 * DV])
        o_sq = sb("o_sq", [P, 8, DV])
        ss = sb("ss", [P, 2, 8])
        ms = sb("ms", [P, 2, 8])
        rms = sb("rms", [P, 2, 8])
        o_tok = sb("o_tok", [P, TB, E])
        o_tr = sb("o_tr", [P, EB, T])
        qkx = sb("qkx", [P, 2, T])
        neg_emax = sb("neg_emax", [P, TB])
        esum = sb("esum", [P, TB])
        erec = sb("erec", [P, TB])
        e_sb = sb("e_sb", [P, TB, T])
        attn_x = sb("attn_x", [P, TB, T])
        attn_xT = sb("attn_xT", [P, TB, T])
        z = sb("z", [P, TB, E])
        stats = sb("stats", [P, TB, 6])
        mv = sb("mv", [P, TB, 2])
        var_eps = sb("var_eps", [P, TB])
        rstd = sb("rstd", [P, TB])
        x1, x2, x3 = (sb(n, [P, TB, E]) for n in ("x1", "x2", "x3"))
        x1T, x2T = sb("x1T", [P, EB, T]), sb("x2T", [P, EB, T])
        th = sb("th", [P, 2, T])
        gated = sb("gated", [P, 2, T])
        hT = sb("hT", [P, FB, T])

        score = [ctx.enter_context(nc.psum_tensor(f"score{i}", [P, 1024], F32)) for i in range(2)]
        x_score, s_score = score
        pv_bank = ctx.enter_context(nc.psum_tensor("pv_bank", [P, 512], F32))
        ta, tb, tc = (ctx.enter_context(nc.psum_tensor(f"t{i}", [P, 512], F32)) for i in "abc")

        names_in = "x_tr0 x_tr1 x_tok ctx_tr wq wk wv wo lam g xw xb wg wu wd".split()
        loaded = {n: sem(f"in_{n}") for n in names_in}
        stack_in = [sem(f"stack_in{i}") for i in range(2)]
        m_rows_in = sem("m_rows_in")
        stored = sem("stored")
        q_zeros, k_ones, zeros_made, v_ones = sem("q_zeros"), sem("k_ones"), sem("zeros_made"), sem("v_ones")
        v_zeros = sem("v_zeros")
        raw_const, ident_made, mask_made, ident_bf_made = sem("raw_const"), sem("ident_made"), sem("mask_made"), sem("ident_bf_made")
        wog_made, lam_dots, lam_exp = sem("wog_made"), sem("lam_dots"), sem("lam_exp")
        q_proj, k_proj, v_proj = sem("q_proj"), sem("k_proj"), sem("v_proj")
        q_out, k_out, v_out = sem("q_out"), sem("k_out"), sem("v_out")
        q_clamped, q_parts, k_parts = sem("q_clamped"), sem("q_parts"), sem("k_parts")
        s_ready, s_max = sem("s_ready"), sem("s_max")
        m_parts, mT_ready, mT_out = sem("m_parts"), sem("mT_ready"), sem("mT_out")
        st_ready, exp_done, masked = sem("st_ready"), sem("exp_done"), sem("masked")
        pv_ready, pv_out, pvT_ready, pvT_used = sem("pv_ready"), sem("pv_out"), sem("pvT_ready"), sem("pvT_used")
        ss_ready, rms_ready, o_ready = sem("ss_ready"), sem("rms_ready"), sem("o_ready")
        qkx_ready, qkx_out = sem("qkx_ready"), sem("qkx_out")
        oT_ready, oT_out, y_ready = sem("oT_ready"), sem("oT_out"), sem("y_ready")
        e_ready, e_max, e_exp, a_ready = sem("e_ready"), sem("e_max"), sem("e_exp"), sem("a_ready")
        aT_ready, aT_out = sem("aT_ready"), sem("aT_out")
        z1_done, z2_done, z3_done = sem("z1_done"), sem("z2_done"), sem("z3_done")
        var_ready, rstd_ready = sem("var_ready"), sem("rstd_ready")
        x1_done, x2_done, x3_done = sem("x1_done"), sem("x2_done"), sem("x3_done")
        x1T_ready, x1T_out, x2T_ready, x2T_out = sem("x1T_ready"), sem("x1T_out"), sem("x2T_ready"), sem("x2T_out")
        xm_ready = sem("xm_ready")
        hid_ready, tanh_done, h_done, down_ready = sem("hid_ready"), sem("tanh_done"), sem("h_done"), sem("down_ready")
        dve_step, pool_step = sem("dve_step"), sem("pool_step")

        block = ctx.enter_context(nc.Block())

        def x_bank(b, u):
            return score[u % 2] if b == B - 1 else x_score

        def hidden_bank(t, j):
            return score[j // 2 % 2][:, 512 * (j % 2):512 * (j % 2) + 512] if t == B - 1 else tc[:]

        def wait_stack(eng, b):
            eng.wait_ge(stack_in[b % 2], 16 * (2 * len(PAIRS) * (b // 2 + 1) + b // 2))

        def wait(eng, s, n):
            if n > 0:
                eng.wait_ge(s, n)

        @block.sync
        def _(sp):
            def load(dst, src, name):
                sp.dma_start(dst, src).then_inc(loaded[name], 16)

            load(x_tr[:, 0], xT[0], "x_tr0")
            load(wq_sb[:], wqT, "wq")
            load(wk_sb[:], wkT, "wk")
            load(wv_sb[:], wvT, "wv")
            load(x_tr[:, 1], xT[1], "x_tr1")
            load(lam_sb[:], lam_in, "lam")
            load(x_tok[:], x[0], "x_tok")
            load(ctx_tr[:], ctxT[0], "ctx_tr")

            def stack(b):
                i = b % 2
                if b < 2:
                    sp.wait_ge(k_ones, b + 1)
                    sp.wait_ge(q_zeros, b + 1)
                sp.wait_ge(k_parts, b + 1)
                if b >= 2:
                    sp.wait_ge(st_ready, H * (b - 1))
                    sp.wait_ge(zeros_made, 1)
                for g, (_, pk) in enumerate(PAIRS):
                    sp.dma_start(k_stacks[i][D * g:D * g + D, :, :], k_part[:, i, pk]).then_inc(stack_in[i], 16)
                if b >= 2:
                    sp.dma_start(q_stacks[i][M_ROW:M_ROW + PARTS, :, :], zeros[:]).then_inc(stack_in[i], 16)
                sp.wait_ge(q_parts, b + 1)
                for g, (pq, _) in enumerate(PAIRS):
                    sp.dma_start(q_stacks[i][D * g:D * g + D, :, :], q_part[:, i, pq]).then_inc(stack_in[i], 16)

            def maxima(b):
                sp.wait_ge(mT_out, b + 1)
                sp.dma_start(q_stacks[b % 2][M_ROW:M_ROW + PARTS, :, :], mT[:]).then_inc(m_rows_in, 16)

            def store(t):
                sp.wait_ge(x3_done, t + 1)
                sp.dma_start(out[t], x3[:]).then_inc(stored, 16)

            stack(0)
            stack(1)
            sp.wait_ge(v_proj, 1)
            load(x_tr[:, 0], xT[2], "x_tr0")
            maxima(0)
            for b in range(B):
                if b >= 2:
                    store(b - 2)
                if b > 0:
                    sp.wait_ge(z1_done, b)
                    load(x_tok[:], x[b], "x_tok")
                if b + 3 < B:
                    sp.wait_ge(v_proj, b + 2)
                    load(x_tr[:, (b + 3) % 2], xT[b + 3], f"x_tr{(b + 3) % 2}")
                if b + 2 < B:
                    stack(b + 2)
                if b + 1 < B:
                    sp.wait_ge(qkx_ready, b + 1)
                    load(ctx_tr[:], ctxT[b + 1], "ctx_tr")
                    maxima(b + 1)
            store(B - 2)
            store(B - 1)
            sp.wait_ge(stored, 16 * B)

        @block.gpsimd
        def _(pool):
            step = [0]

            def link(ins):
                step[0] += 1
                ins.then_inc(pool_step, 1)
                pool.wait_ge(pool_step, step[0])

            def ones_in_k(i):
                nc.gpsimd.memset(k_stacks[i][:].bitcast(U32), 0x3F803F80).then_inc(k_ones, 1)

            nc.gpsimd.memset(ident[:], 0.0).then_inc(raw_const, 1)
            nc.gpsimd.memset(mask[:], 0.0).then_inc(raw_const, 1)
            ones_in_k(0)
            nc.gpsimd.memset(half_power[:], -0.5).then_inc(raw_const, 1)
            pool.wait_ge(raw_const, 3)
            nc.gpsimd.affine_select(out=ident[:], in_=ident[:], compare_op=ALU.not_equal, fill=1.0, base=0,
                                    pattern=[[-1, P]], channel_multiplier=1).then_inc(ident_made, 1)
            nc.gpsimd.affine_select(out=mask[:], in_=mask[:], compare_op=ALU.is_ge, fill=MASKED, base=0,
                                    pattern=[[0, 4], [-1, P]], channel_multiplier=1).then_inc(mask_made, 1)

            def q_split(b):
                pool.wait_ge(q_clamped, b + 1)
                if b >= 2:
                    wait_stack(pool, b - 2)
                q, part = qk[:, 0], q_part[:, b % 2]
                link(nc.gpsimd.tensor_scalar(part[:, 0], q, 1.0, 0.0, ALU.mult, ALU.add))
                link(nc.gpsimd.tensor_tensor(q, q, part[:, 0], ALU.subtract))
                link(nc.gpsimd.tensor_scalar(part[:, 1], q, 1.0, 0.0, ALU.mult, ALU.add))
                link(nc.gpsimd.tensor_tensor(q, q, part[:, 1], ALU.subtract))
                nc.gpsimd.tensor_scalar(part[:, 2], q, 1.0, 0.0, ALU.mult, ALU.add).then_inc(q_parts, 1)

            def layer_rstd(t, n):
                pool.wait_ge(var_ready, 3 * t + n + 1)
                link(nc.gpsimd.tensor_scalar(var_eps[:], mv[:, :, 1], 1.0, EPS, ALU.mult, ALU.add))
                nc.gpsimd.tensor_tensor(rstd[:], var_eps[:], half_power[:, 0:TB], ALU.pow).then_inc(rstd_ready, 1)

            def causal(b, u):
                pool.wait_ge(exp_done, H * b + u + 1)
                p = prob[:, u % RING, :]
                first = p[:, 0:512].rearrange("p (c q) -> p c q", c=2)[:, :, 0:P]
                nc.gpsimd.affine_select(out=first, in_=first, compare_op=ALU.is_ge, fill=0.0, base=0,
                                        pattern=[[0, 2], [1, P]], channel_multiplier=-1)
                second = p[:, 512:768].rearrange("p (c q) -> p c q", c=2)
                nc.gpsimd.affine_select(out=second, in_=second, compare_op=ALU.is_ge, fill=0.0, base=0,
                                        pattern=[[0, 2], [1, P]], channel_multiplier=-1).then_inc(masked, 1)

            def head_rms(b, quad):
                pool.wait_ge(ss_ready, QUADS * b + quad + 1)
                s = quad % 2
                link(nc.gpsimd.tensor_scalar(ms[:, s], ss[:, s], 1.0 / DV, EPS, ALU.mult, ALU.add))
                nc.gpsimd.tensor_tensor(rms[:, s], ms[:, s], half_power[:], ALU.pow).then_inc(rms_ready, 1)

            def body(b):
                t, tail = b - 1, b > 0
                causal(b, 0)
                causal(b, 1)
                if b >= 2:
                    layer_rstd(t - 1, 2)
                causal(b, 2)
                causal(b, 3)
                if tail:
                    layer_rstd(t, 0)
                causal(b, 4)
                causal(b, 5)
                if b + 2 < B:
                    q_split(b + 2)
                causal(b, 6)
                head_rms(b, 0)
                causal(b, 7)
                causal(b, 8)
                if tail:
                    layer_rstd(t, 1)
                causal(b, 9)
                causal(b, 10)
                head_rms(b, 1)
                for u in range(11, 14):
                    causal(b, u)
                head_rms(b, 2)
                causal(b, 14)
                causal(b, 15)
                head_rms(b, 3)

            q_split(0)
            ones_in_k(1)
            q_split(1)
            nc.gpsimd.memset(zeros[:], 0.0).then_inc(zeros_made, 1)
            for b in range(B):
                body(b)
            layer_rstd(B - 2, 2)
            for n in range(3):
                layer_rstd(B - 1, n)

        @block.scalar
        def _(act):
            def load(dst, src, name):
                act.dma_start(dst, src).then_inc(loaded[name], 16)

            load(wo_sb[:], woT, "wo")
            load(g_sb[:], g_in, "g")
            load(xw_sb[:], xwT, "xw")
            load(xb_sb[:], xb, "xb")
            load(wg_sb[:], wgT, "wg")
            load(wu_sb[:], wuT, "wu")
            load(wd_sb[:], wdT, "wd")
            def flat(t):
                return t.rearrange("p a b -> p (a b)")

            def q_copy(b, bank):
                act.wait_ge(q_proj, b + 1)
                wait(act, q_parts, b)
                nc.scalar.activation(flat(qk[:, 0]), bank, ACT.Copy, scale=SCALING).then_inc(q_out, 1)

            def k_copy(b, bank):
                act.wait_ge(k_proj, b + 1)
                wait(act, k_parts, b)
                nc.scalar.activation(flat(qk[:, 1]), bank, ACT.Copy).then_inc(k_out, 1)

            def v_copy(b, bank):
                act.wait_ge(v_proj, b + 1)
                wait(act, pv_ready, QUADS * (b - 2))
                nc.scalar.activation(v_sb[:, b % 3, :, :, 0:DV], bank.rearrange("p (a h d) -> p a h d", a=TB, h=H),
                                     ACT.Copy).then_inc(v_out, 1)

            def qkx_copy(t):
                act.wait_ge(qkx_ready, t + 1)
                if t == 0:
                    act.wait_ge(loaded["xb"], 16)
                for i in range(2):
                    nc.scalar.activation(qkx[:, i], ta[:, T * i:T * i + T], ACT.Identity,
                                         bias=xb_sb[:, i:i + 1]).then_inc(qkx_out, 1)

            def copy_out(t, dst, bank, ready, done):
                act.wait_ge(ready, t + 1)
                nc.scalar.activation(flat(dst[:]), bank[:], ACT.Copy).then_inc(done, 1)

            def energy_exp(t):
                act.wait_ge(e_max, t + 1)
                for i in range(TB):
                    nc.scalar.activation(e_sb[:, i], tb[:, T * i:T * i + T], ACT.Exp, bias=neg_emax[:, i:i + 1],
                                         accum_out=esum[:, i:i + 1]).then_inc(e_exp, 1)

            def tanh_gate(t, j, bank):
                act.wait_ge(hid_ready, FB * t + j + 1)
                wait(act, h_done, FB * t + j - 1)
                nc.scalar.activation(th[:, j % 2], bank[:, 0:T], ACT.Tanh, scale=0.5).then_inc(tanh_done, 1)

            def m_out(b):
                act.wait_ge(mT_ready, b + 1)
                wait(act, m_rows_in, 16 * b)
                nc.scalar.activation(mT[:], pv_bank[0:PARTS * N2, 0:T // 2].bitcast(BF16), ACT.Copy).then_inc(mT_out, 1)

            def prob_exp(b, u):
                act.wait_ge(st_ready, H * b + u + 1)
                wait(act, pv_ready, QUADS * b + u // 4 - 1)
                nc.scalar.activation(prob[:, u % RING, :], x_bank(b, u)[:, 0:768], ACT.Exp).then_inc(exp_done, 1)

            def pv_copy(b, quad):
                act.wait_ge(pv_ready, QUADS * b + quad + 1)
                wait(act, pvT_ready, QUADS * b + quad - 1)
                nc.scalar.activation(oT[:, quad % 2], pv_bank[:], ACT.Copy).then_inc(pv_out, 1)

            def body(b):
                t, tail, far = b - 1, b > 0, b + 2 < B

                def tanh(j):
                    if tail:
                        tanh_gate(t, j, tc)

                prob_exp(b, 0)
                if tail:
                    copy_out(t, o_tr, ta, oT_ready, oT_out)
                prob_exp(b, 1)
                prob_exp(b, 2)
                prob_exp(b, 3)
                if far:
                    q_copy(b + 2, tb[:])
                prob_exp(b, 4)
                pv_copy(b, 0)
                prob_exp(b, 5)
                if tail:
                    copy_out(t, x1T, ta, x1T_ready, x1T_out)
                if far:
                    k_copy(b + 2, tc[:])
                prob_exp(b, 6)
                prob_exp(b, 7)
                if far:
                    v_copy(b + 2, tc[:])
                prob_exp(b, 8)
                if tail:
                    copy_out(t, x2T, ta, x2T_ready, x2T_out)
                prob_exp(b, 9)
                pv_copy(b, 1)
                tanh(0)
                prob_exp(b, 10)
                tanh(1)
                prob_exp(b, 11)
                tanh(2)
                prob_exp(b, 12)
                pv_copy(b, 2)
                tanh(3)
                prob_exp(b, 13)
                tanh(4)
                prob_exp(b, 14)
                qkx_copy(b)
                tanh(5)
                prob_exp(b, 15)
                tanh(6)
                energy_exp(b)
                pv_copy(b, 3)
                tanh(7)
                if b + 1 < B:
                    m_out(b + 1)
                copy_out(b, attn_xT, ta, aT_ready, aT_out)

            q_copy(0, ta[:])
            k_copy(0, tb[:])
            act.wait_ge(v_ones, 1)
            v_copy(0, tc[:])
            q_copy(1, x_score[:, 0:512])
            k_copy(1, x_score[:, 512:1024])
            v_copy(1, s_score[:, 0:512])
            act.wait_ge(lam_dots, 1)
            nc.scalar.activation(lam_e[:], lam_d[:], ACT.Exp).then_inc(lam_exp, 1)
            m_out(0)
            for b in range(B):
                body(b)
            t = B - 1
            copy_out(t, o_tr, ta, oT_ready, oT_out)
            copy_out(t, x1T, ta, x1T_ready, x1T_out)
            copy_out(t, x2T, ta, x2T_ready, x2T_out)
            for j in range(FB):
                tanh_gate(t, j, hidden_bank(t, j))

        @block.tensor
        def _(pe):
            def matmuls(out_ap, pairs):
                for n, (lhsT, rhs) in enumerate(pairs):
                    mm = nc.tensor.matmul(out_ap, lhsT, rhs, start=(n == 0), stop=(n == len(pairs) - 1))
                return mm

            def blk(i):
                return slice(P * i, P * i + P)

            def project_qk(b, bank, w, done):
                pe.wait_ge(loaded[f"x_tr{b % 2}"], 16 * (b // 2 + 1))
                for half in range(2):
                    mm = matmuls(bank[:, T * half:T * half + T],
                                 [(w[:, e, blk(half)], x_tr[:, b % 2, e, :]) for e in range(EB)])
                mm.then_inc(done, 1)

            def project_v(b, bank):
                for i in range(TB):
                    mm = matmuls(bank[:, E * i:E * i + E], [(x_tr[:, b % 2, e, blk(i)], wv_sb[:, e, :]) for e in range(EB)])
                mm.then_inc(v_proj, 1)

            def four_transposes(bank, src):
                for i in range(2):
                    for j in range(2):
                        mm = nc.tensor.transpose(bank[:, T * j + P * i:T * j + P * i + P], src[:, i, blk(j)], ident[:])
                return mm

            def heads_transposed(t):
                pe.wait_ge(o_ready, QUADS * (t + 1))
                pe.wait_ge(aT_out, t + 1)
                four_transposes(ta, o_tok).then_inc(oT_ready, 1)

            def project_out(t):
                pe.wait_ge(oT_out, t + 1)
                if t == 0:
                    pe.wait_ge(wog_made, 2)
                for i in range(TB):
                    mm = matmuls(ta[:, E * i:E * i + E], [(o_tr[:, e, blk(i)], wog[:, e, :]) for e in range(EB)])
                mm.then_inc(y_ready, 1)

            def x1_transposed(t):
                pe.wait_ge(x1_done, t + 1)
                four_transposes(ta, x1).then_inc(x1T_ready, 1)

            def cross(t):
                pe.wait_ge(x1T_out, t + 1)
                for i in range(TB):
                    mm = matmuls(ta[:, T * i:T * i + T], [(x1T[:, n, blk(i)], attn_xT[:, n, :]) for n in range(TB)])
                mm.then_inc(xm_ready, 1)

            def x2_transposed(t):
                pe.wait_ge(x2_done, t + 1)
                four_transposes(ta, x2).then_inc(x2T_ready, 1)

            def cross_qk(b):
                pe.wait_ge(loaded["ctx_tr"], 16 * (b + 1))
                if b == 0:
                    pe.wait_ge(loaded["xw"], 16)
                pe.wait_ge(pvT_used, QUADS * b + 3)
                for i in range(2):
                    mm = nc.tensor.matmul(ta[:, T * i:T * i + T], xw_sb[:, i, :], ctx_tr[:], start=True, stop=True)
                mm.then_inc(qkx_ready, 1)

            def energy(b):
                pe.wait_ge(qkx_out, 2 * (b + 1))
                pe.wait_ge(pvT_used, QUADS * b + 2)
                for i in range(TB):
                    mm = nc.tensor.matmul(tb[:, T * i:T * i + T], qkx[:, 0, blk(i)], qkx[:, 1, :], start=True, stop=True)
                mm.then_inc(e_ready, 1)

            def cross_transposed(b):
                pe.wait_ge(a_ready, b + 1)
                pe.wait_ge(pvT_used, QUADS * (b + 1))
                four_transposes(ta, attn_x).then_inc(aT_ready, 1)

            def hidden(t, j):
                bank = hidden_bank(t, j)
                if j == 0:
                    pe.wait_ge(x2T_out, t + 1)
                    if t == 0:
                        pe.wait_ge(loaded["wg"], 16)
                        pe.wait_ge(loaded["wu"], 16)
                if t == B - 1:
                    pe.wait_ge(exp_done, H * B)
                    wait(pe, h_done, FB * t + j - 3)
                elif j == 0:
                    pe.wait_ge(v_out, min(t + 4, B))
                    wait(pe, h_done, FB * t)
                else:
                    pe.wait_ge(h_done, FB * t + j)
                for n, w in enumerate((wg_sb, wu_sb)):
                    mm = matmuls(bank[:, T * n:T * n + T], [(w[:, e, blk(j)], x2T[:, e, :]) for e in range(EB)])
                mm.then_inc(hid_ready, 1)

            def down(t, j):
                pe.wait_ge(h_done, FB * t + j + 1)
                if t == 0 and j == 0:
                    pe.wait_ge(loaded["wd"], 16)
                if j == 0:
                    pe.wait_ge(e_exp, TB * min(t + 2, B))
                for i in range(TB):
                    mm = nc.tensor.matmul(tb[:, E * i:E * i + E], hT[:, j, blk(i)], wd_sb[:, j, :],
                                          start=(j == 0 and i == 0), stop=(j == FB - 1), skip_group_check=True)
                if j == FB - 1:
                    mm.then_inc(down_ready, 1)

            def scores(b, u, s):
                if u == 0:
                    wait_stack(pe, b)
                    if b == 0:
                        pe.wait_ge(q_out, 2)
                        pe.wait_ge(k_out, 2)
                        pe.wait_ge(v_out, 2)
                        pe.wait_ge(ident_bf_made, 1)
                        pe.wait_ge(mask_made, 1)
                if b == 0:
                    wait(pe, s_max, u - 1)
                else:
                    pe.wait_ge(s_max, H * b + u)
                first = True
                for m in range(2):
                    n = 2 * u + m
                    for q, k, col in ((0, 0, P * m), (1, 1, 256 + P * m), (1, 0, 512 + P * m)):
                        nc.tensor.matmul(s[:, col:col + P], q_stacks[b % 2][:, n, blk(q)], k_stacks[b % 2][:, n, blk(k)],
                                         start=(first or (col == 512)), stop=(col >= 512), skip_group_check=True)
                        first = False
                nc.tensor.matmul(s[:, 0:512], ident_bf[:], mask[:].rearrange("p a b -> p (a b)"),
                                 start=False, stop=True, skip_group_check=True).then_inc(s_ready, 1)

            def maxima_transposed(b):
                pe.wait_ge(m_parts, b + 1)
                wait(pe, pv_out, QUADS * b)
                for i in range(TB):
                    mm = nc.tensor.transpose(pv_bank[0:PARTS * N2, 64 * i:64 * i + 64].bitcast(BF16),
                                             m_part[:, i].rearrange("p a b -> p (a b)"), ident_bf[:])
                mm.then_inc(mT_ready, 1)

            def scores_transposed(b, u):
                if u == 0:
                    pe.wait_ge(m_rows_in, 16 * (b + 1))
                wait(pe, exp_done, H * b + u - (1 if b == B - 1 and u > 0 else 0))
                s = x_bank(b, u)
                q_stack, k_stack = q_stacks[b % 2], k_stacks[b % 2]
                for m in range(2):
                    n = 2 * u + m
                    nc.tensor.matmul(s[:, T * m:T * m + T], k_stack[:, n, blk(0)], q_stack[:, n, :],
                                     start=True, stop=True)
                for m in range(2):
                    n = 2 * u + m
                    mm = nc.tensor.matmul(s[:, 512 + P * m:512 + P * m + P], k_stack[:, n, blk(1)],
                                          q_stack[:, n, blk(1)], start=True, stop=True)
                mm.then_inc(st_ready, 1)

            def times_v(b, quad):
                pe.wait_ge(masked, H * b + 4 * quad + 4)
                if quad == 0:
                    pe.wait_ge(v_out, b + 1)
                    pe.wait_ge(mT_out, b + 1)
                wait(pe, pv_out, QUADS * b + quad)
                for i in range(4):
                    h = 4 * quad + i
                    nc.tensor.matmul(pv_bank[32 * i:32 * i + 32, :], v_sb[:, b % 3, 0, h, :], prob[:, h % RING, 0:512],
                                     start=True, stop=False)
                for i in range(4):
                    h = 4 * quad + i
                    late = pv_bank[32 * i:32 * i + 32, :].rearrange("p (m q) -> p m q", m=2)[:, :, P:T]
                    mm = nc.tensor.matmul(late, v_sb[:, b % 3, 1, h, :], prob[:, h % RING, 512:768].rearrange("p (m q) -> p m q", m=2),
                                          start=False, stop=True)
                mm.then_inc(pv_ready, 1)

            def pv_transposed(b, quad):
                pe.wait_ge(pv_out, QUADS * b + quad + 1)
                if quad == 0:
                    pe.wait_ge(q_out, min(b + 3, B))
                    wait(pe, z3_done, b - 1)
                elif quad == 1:
                    pe.wait_ge(pvT_used, QUADS * b + 1)
                elif quad == 2:
                    wait(pe, x2T_out, b)
                    wait(pe, aT_out, b)
                else:
                    pe.wait_ge(qkx_out, 2 * (b + 1))
                bank = tb if quad < 2 else ta
                for i in range(4):
                    mm = nc.tensor.transpose(bank[:, blk(i)], oT[:, quad % 2, blk(i)], ident[:])
                mm.then_inc(pvT_ready, 1)

            def next_q(b):
                wait(pe, z3_done, b - 3)
                project_qk(b, tb, wq_sb, q_proj)

            def next_k(b):
                wait(pe, h_done, FB * (b - 3))
                project_qk(b, tc, wk_sb, k_proj)

            def next_v(b):
                pe.wait_ge(k_out, b + 1)
                project_v(b, tc)

            def body(b):
                t = b - 1
                tail, ahead, far = b > 0, b + 1 < B, b + 2 < B

                def x_head(u):
                    scores_transposed(b, u)

                def s_head(u):
                    if ahead:
                        scores(b + 1, u, s_score)

                def feed(j):
                    if tail:
                        hidden(t, j)

                x_head(0)
                if tail:
                    heads_transposed(t)
                s_head(0)
                x_head(1)
                s_head(1)
                if tail:
                    project_out(t)
                x_head(2)
                s_head(2)
                x_head(3)
                if far:
                    next_q(b + 2)
                x_head(4)
                s_head(3)
                times_v(b, 0)
                x_head(5)
                if tail:
                    x1_transposed(t)
                s_head(4)
                if far:
                    next_k(b + 2)
                x_head(6)
                s_head(5)
                pv_transposed(b, 0)
                if tail:
                    cross(t)
                x_head(7)
                s_head(6)
                if far:
                    next_v(b + 2)
                x_head(8)
                s_head(7)
                if tail:
                    x2_transposed(t)
                x_head(9)
                times_v(b, 1)
                feed(0)
                x_head(10)
                s_head(8)
                pv_transposed(b, 1)
                feed(1)
                x_head(11)
                s_head(9)
                feed(2)
                x_head(12)
                times_v(b, 2)
                s_head(10)
                feed(3)
                x_head(13)
                pv_transposed(b, 2)
                s_head(11)
                feed(4)
                x_head(14)
                s_head(12)
                cross_qk(b)
                feed(5)
                x_head(15)
                s_head(13)
                energy(b)
                feed(6)
                s_head(14)
                times_v(b, 3)
                feed(7)
                s_head(15)
                pv_transposed(b, 3)
                if tail:
                    for j in range(4):
                        down(t, j)
                if ahead:
                    maxima_transposed(b + 1)
                if tail:
                    down(t, 4)
                    down(t, 5)
                cross_transposed(b)
                if tail:
                    down(t, 6)
                    down(t, 7)

            for b, (q_bank, k_bank, v_bank) in enumerate((
                    (ta, tb, tc), (x_score[:, 0:512], x_score[:, 512:1024], s_score[:, 0:512]))):
                pe.wait_ge(loaded["wq"], 16)
                project_qk(b, q_bank, wq_sb, q_proj)
                pe.wait_ge(loaded["wk"], 16)
                project_qk(b, k_bank, wk_sb, k_proj)
                pe.wait_ge(loaded["wv"], 16)
                project_v(b, v_bank)
            for u in range(H):
                scores(0, u, score[u % 2])
            maxima_transposed(0)
            for b in range(B):
                body(b)
            t = B - 1
            heads_transposed(t)
            project_out(t)
            x1_transposed(t)
            cross(t)
            x2_transposed(t)
            for j in range(FB):
                hidden(t, j)
                if j > 1:
                    down(t, j - 2)
            down(t, FB - 2)
            down(t, FB - 1)

        @block.vector
        def _(dve):
            step = [0]

            def link(ins):
                step[0] += 1
                ins.then_inc(dve_step, 1)
                dve.wait_ge(dve_step, step[0])

            def zeros_in_q(i):
                nc.vector.memset(q_stacks[i][:].bitcast(U32), 0).then_inc(q_zeros, 1)

            def clamp_q(b):
                dve.wait_ge(q_out, b + 1)
                nc.vector.tensor_scalar(qk[:, 0], qk[:, 0], -LIMIT, LIMIT, ALU.max, ALU.min).then_inc(q_clamped, 1)

            def split_k(b):
                dve.wait_ge(k_out, b + 1)
                k = qk[:, 1]
                link(nc.vector.tensor_scalar(k, k, -LIMIT, LIMIT, ALU.max, ALU.min))
                if b >= 2:
                    wait_stack(dve, b - 2)
                part = k_part[:, b % 2]
                link(nc.vector.tensor_copy(part[:, 0], k))
                link(nc.vector.tensor_tensor(k, k, part[:, 0], ALU.subtract))
                link(nc.vector.tensor_copy(part[:, 1], k))
                link(nc.vector.tensor_tensor(k, k, part[:, 1], ALU.subtract))
                nc.vector.tensor_copy(part[:, 2], k).then_inc(k_parts, 1)

            def score_max(b, u, s):
                dve.wait_ge(s_ready, H * b + u + 1)
                nc.vector.tensor_reduce(nmax6[:, u, :], s[:, 0:768].rearrange("p (a k) -> p a k", k=P),
                                        AX.X, ALU.max, negate=True).then_inc(s_max, 1)

            def split_maxima(b):
                dve.wait_ge(s_max, H * (b + 1))
                wait(dve, mT_ready, b)
                nc.vector.tensor_copy(nmax[:, 0, :].rearrange("p (h m) -> p h m", m=2), nmax6[:, :, 0:2])
                link(nc.vector.tensor_tensor(nmax[:, 1, :].rearrange("p (h m) -> p h m", m=2), nmax6[:, :, 2:4],
                                             nmax6[:, :, 4:6], ALU.min))
                link(nc.vector.tensor_copy(m_part[:, :, 0], nmax[:]))
                link(nc.vector.tensor_tensor(m_rest[:], nmax[:], m_part[:, :, 0], ALU.subtract))
                link(nc.vector.tensor_copy(m_part[:, :, 1], m_rest[:]))
                link(nc.vector.tensor_tensor(m_rest[:], m_rest[:], m_part[:, :, 1], ALU.subtract))
                nc.vector.tensor_copy(m_part[:, :, 2], m_rest[:]).then_inc(m_parts, 1)

            def combine(b, quad):
                s = quad % 2
                dve.wait_ge(pvT_ready, QUADS * b + quad + 1)
                bank = tb if quad < 2 else ta
                maps = bank[:].rearrange("p (m r c) -> p m r c", m=2, c=32)
                rs = rsum[:, 0:2, :]
                link(nc.vector.reciprocal(rs, maps[:, :, :, DV]))
                for m in range(2):
                    ins = nc.vector.tensor_tensor(a_map[:, s, m].rearrange("p (r c) -> p r c", c=DV), maps[:, m, :, 0:DV],
                                                  rsum[:, m, :].unsqueeze(2).to_broadcast([P, 8, DV]), ALU.mult)
                ins.then_inc(pvT_used, 1)
                dve.wait_ge(pvT_used, QUADS * b + quad + 1)
                o = o_q[:, s].rearrange("p a b -> p (a b)")
                link(nc.vector.scalar_tensor_tensor(out=o, in0=a_map[:, s, 1], scalar=neg_lam[:, 0:1],
                                                    in1=a_map[:, s, 0], op0=ALU.mult, op1=ALU.add))
                link(nc.vector.tensor_tensor(o_sq[:].rearrange("p r c -> p (r c)"), o, o, ALU.mult))
                nc.vector.tensor_reduce(ss[:, s], o_sq[:], AX.X, ALU.add).then_inc(ss_ready, 1)

            def normalise(b, quad):
                s = quad % 2
                dve.wait_ge(rms_ready, QUADS * b + quad + 1)
                wait(dve, oT_ready, b)
                for i in range(TB):
                    ins = nc.vector.tensor_tensor(
                        o_tok[:, i, 4 * DV * quad:4 * DV * (quad + 1)].rearrange("p (h c) -> p h c", c=DV),
                        o_q[:, s, i].rearrange("p (h c) -> p h c", c=DV),
                        rms[:, s, 4 * i:4 * i + 4].unsqueeze(2).to_broadcast([P, 4, DV]), ALU.mult)
                ins.then_inc(o_ready, 1)

            def layer_stats():
                for i in range(TB):
                    ins = nc.vector.bn_stats(stats[:, i], z[:, i])
                link(ins)
                for i in range(TB):
                    ins = nc.vector.bn_aggr(mv[:, i], stats[:, i])
                ins.then_inc(var_ready, 1)

            def layer_norm(t, n, dst, done):
                dve.wait_ge(rstd_ready, 3 * t + n + 1)
                for i in range(TB):
                    ins = nc.vector.tensor_scalar(dst[:, i], z[:, i], mv[:, i, 0:1], rstd[:, i:i + 1],
                                                  ALU.subtract, ALU.mult)
                ins.then_inc(done, 1)

            def flat(t):
                return t.rearrange("p a b -> p (a b)")

            def energy_max(t):
                dve.wait_ge(e_ready, t + 1)
                nc.vector.tensor_reduce(neg_emax[:], tb[:].rearrange("p (a k) -> p a k", a=TB), AX.X, ALU.max,
                                        negate=True).then_inc(e_max, 1)

            def cross_weights(t):
                dve.wait_ge(e_exp, TB * (t + 1))
                link(nc.vector.reciprocal(erec[:], esum[:]))
                for i in range(TB):
                    ins = nc.vector.tensor_scalar(attn_x[:, i], e_sb[:, i], erec[:, i:i + 1], None, ALU.mult)
                ins.then_inc(a_ready, 1)

            def first_residual(t):
                wait(dve, x3_done, t)
                dve.wait_ge(y_ready, t + 1)
                dve.wait_ge(loaded["x_tok"], 16 * (t + 1))
                nc.vector.tensor_tensor(flat(z[:]), ta[:], flat(x_tok[:]), ALU.add).then_inc(z1_done, 1)
                dve.wait_ge(z1_done, t + 1)
                layer_stats()

            def second_residual(t):
                dve.wait_ge(xm_ready, t + 1)
                nc.vector.tensor_tensor(flat(z[:]), ta[:], flat(x1[:]), ALU.add).then_inc(z2_done, 1)
                dve.wait_ge(z2_done, t + 1)
                layer_stats()

            def gate(t, j, bank):
                dve.wait_ge(tanh_done, FB * t + j + 1)
                link(nc.vector.scalar_tensor_tensor(out=gated[:, j % 2], in0=th[:, j % 2], scalar=1.0,
                                                    in1=bank[:, 0:T], op0=ALU.add, op1=ALU.mult))
                nc.vector.tensor_tensor(hT[:, j], gated[:, j % 2], bank[:, T:2 * T], ALU.mult).then_inc(h_done, 1)

            def third_residual(t):
                dve.wait_ge(down_ready, t + 1)
                nc.vector.scalar_tensor_tensor(out=flat(z[:]), in0=tb[:], scalar=0.5, in1=flat(x2[:]), op0=ALU.mult,
                                               op1=ALU.add).then_inc(z3_done, 1)
                dve.wait_ge(z3_done, t + 1)
                layer_stats()

            def result(t):
                wait(dve, stored, 16 * t)
                layer_norm(t, 2, x3, x3_done)

            def late_constants():
                dve.wait_ge(lam_exp, 1)
                link(nc.vector.scalar_tensor_tensor(out=neg_lam[:], in0=lam_e[:, 1:2], scalar=LAMBDA_INIT,
                                                    in1=lam_e[:, 0:1], op0=ALU.subtract, op1=ALU.subtract))
                dve.wait_ge(loaded["wo"], 16)
                dve.wait_ge(loaded["g"], 16)
                for e in range(EB):
                    nc.vector.tensor_scalar(wog[:, e], wo_sb[:, e], g_sb[:, e:e + 1], 1.0 - LAMBDA_INIT,
                                            ALU.mult, ALU.mult).then_inc(wog_made, 1)

            def body(b):
                t = b - 1
                tail, ahead, far = b > 0, b + 1 < B, b + 2 < B

                def next_max(u):
                    if ahead:
                        score_max(b + 1, u, s_score)

                def feed(j):
                    if tail:
                        gate(t, j, tc)

                next_max(0)
                if b >= 2:
                    third_residual(t - 1)
                next_max(1)
                if b >= 2:
                    result(t - 1)
                if tail:
                    first_residual(t)
                next_max(2)
                if tail:
                    layer_norm(t, 0, x1, x1_done)
                if far:
                    clamp_q(b + 2)
                next_max(3)
                next_max(4)
                if far:
                    split_k(b + 2)
                next_max(5)
                combine(b, 0)
                if tail:
                    second_residual(t)
                next_max(6)
                normalise(b, 0)
                if tail:
                    layer_norm(t, 1, x2, x2_done)
                next_max(7)
                feed(0)
                next_max(8)
                combine(b, 1)
                feed(1)
                next_max(9)
                normalise(b, 1)
                feed(2)
                next_max(10)
                feed(3)
                combine(b, 2)
                next_max(11)
                feed(4)
                normalise(b, 2)
                next_max(12)
                feed(5)
                next_max(13)
                energy_max(b)
                feed(6)
                next_max(14)
                feed(7)
                next_max(15)
                if ahead:
                    split_maxima(b + 1)
                combine(b, 3)
                cross_weights(b)
                normalise(b, 3)

            zeros_in_q(0)
            nc.vector.memset(v_sb[:], 0.0).then_inc(v_zeros, 1)
            dve.wait_ge(v_zeros, 1)
            nc.vector.memset(v_sb[:, :, :, :, DV:DV + 1], 1.0).then_inc(v_ones, 1)
            clamp_q(0)
            split_k(0)
            dve.wait_ge(ident_made, 1)
            nc.vector.tensor_copy(ident_bf[:], ident[:]).then_inc(ident_bf_made, 1)
            clamp_q(1)
            split_k(1)
            zeros_in_q(1)
            dve.wait_ge(loaded["lam"], 16)
            nc.vector.tensor_tensor_reduce(lam_w[:, 0], lam_sb[:, 0], lam_sb[:, 1], 1.0, 0.0, ALU.mult, ALU.add,
                                           lam_d[:, 0:1])
            nc.vector.tensor_tensor_reduce(lam_w[:, 1], lam_sb[:, 2], lam_sb[:, 3], 1.0, 0.0, ALU.mult, ALU.add,
                                           lam_d[:, 1:2]).then_inc(lam_dots, 1)
            for u in range(H):
                score_max(0, u, score[u % 2])
            split_maxima(0)
            late_constants()
            for b in range(B):
                body(b)
            t = B - 1
            third_residual(t - 1)
            result(t - 1)
            first_residual(t)
            layer_norm(t, 0, x1, x1_done)
            second_residual(t)
            layer_norm(t, 1, x2, x2_done)
            for j in range(FB):
                gate(t, j, hidden_bank(t, j))
            third_residual(t)
            result(t)


def kernel(x, ctx_1024, L0_attn_Wq, L0_attn_Wk, L0_attn_Wv, L0_attn_Wo, L0_attn_lambda_q1, L0_attn_lambda_k1,
           L0_attn_lambda_q2, L0_attn_lambda_k2, L0_attn_subln_weight, L0_xattn_Wq, L0_xattn_bq, L0_xattn_Wk,
           L0_xattn_bk, L0_ffn_w_gate, L0_ffn_w_up, L0_ffn_w_down):
    import concourse.bacc as bacc
    import numpy as np
    from concourse.bass_utils import run_bass_kernel_spmd

    def rows(a, n):
        a = np.asarray(a)
        return np.ascontiguousarray(a.reshape(n, P, -1).transpose(1, 0, 2))

    def half_heads(w):
        return np.asarray(w).reshape(H, 2, D, E).transpose(1, 2, 0, 3).reshape(E, E)

    x = np.asarray(x)
    context = np.asarray(ctx_1024)
    arrays = {
        "x": np.stack([rows(x[b], TB) for b in range(B)]),
        "xT": np.stack([rows(x[b].T, EB) for b in range(B)]),
        "ctxT": np.ascontiguousarray(context.transpose(0, 2, 1)),
        "wqT": rows(half_heads(L0_attn_Wq).T, EB),
        "wkT": rows(half_heads(L0_attn_Wk).T, EB),
        "wvT": rows(np.asarray(L0_attn_Wv).T, EB),
        "woT": rows(np.asarray(L0_attn_Wo).T, EB),
        "lam_in": np.ascontiguousarray(np.broadcast_to(np.stack([
            np.asarray(a) for a in (L0_attn_lambda_q1, L0_attn_lambda_k1, L0_attn_lambda_q2, L0_attn_lambda_k2)]),
            (P, 4, D))),
        "g_in": np.ascontiguousarray(np.tile(np.asarray(L0_attn_subln_weight), H).reshape(EB, P).T),
        "xwT": np.ascontiguousarray(np.stack([np.asarray(L0_xattn_Wq).T, np.asarray(L0_xattn_Wk).T], 1)),
        "xb": np.ascontiguousarray(np.stack([np.asarray(L0_xattn_bq), np.asarray(L0_xattn_bk)], 1)),
        "wgT": rows(np.asarray(L0_ffn_w_gate).T, EB),
        "wuT": rows(np.asarray(L0_ffn_w_up).T, EB),
        "wdT": rows(np.asarray(L0_ffn_w_down).T, FB),
    }
    nc = bacc.Bacc("TRN2", target_bir_lowering=False, num_devices=1)
    ins = [nc.dram_tensor(n, a.shape, mybir.dt.from_np(a.dtype), kind="ExternalInput").ap() for n, a in arrays.items()]
    out = nc.dram_tensor("out", (B, P, TB, E), F32, kind="ExternalOutput").ap()
    decoder_layer(nc, *ins, out)
    got = run_bass_kernel_spmd(nc, [arrays], core_ids=[0]).results[0]["out"]
    return np.ascontiguousarray(got.transpose(0, 2, 1, 3)).reshape(B, T, E)
```

```python
import math
from contextlib import ExitStack

import concourse.bass as bass
from concourse import mybir
from concourse.alu_op_type import AluOpType as ALU

ACT = mybir.ActivationFunctionType
AX = mybir.AxisListType
F32 = mybir.dt.float32
BF16 = mybir.dt.bfloat16
F32R = mybir.dt.float32r
U32 = mybir.dt.uint32

P = 128
B, T, E = 4, 256, 256
TB, EB = T // P, E // P
H = 16
N2 = 2 * H
D = E // N2
DV = 2 * D
C = 128
F = 1024
FB = F // P
PARTS = 3
PAIRS = ((0, 0), (0, 1), (1, 0), (1, 1), (0, 2), (2, 0))
M_ROW = D * len(PAIRS)
QUADS = H // 4
RING = 6
HELD = 4
WARM_UP = 4
SPLIT_AT = 0
EARLY = 3
LAMBDA_INIT = 0.8 - 0.6 * math.exp(-0.3 * 12)
SCALING = D ** -0.5
EPS = 1e-5
MASKED = -3.0e38
LIMIT = 6.0e18


def decoder_layer(nc, x, xT, ctxT, wqT, wkT, wvT, woT, lam_in, g_in, xwT, xb, wgT, wuT, wdT, out):
    with ExitStack() as ctx:
        def sb(name, shape, dt=F32):
            return ctx.enter_context(nc.sbuf_tensor(name, shape, dt))

        def sem(name):
            return ctx.enter_context(nc.semaphore(name))

        wq_sb, wk_sb, wv_sb, wo_sb = (sb(n, [P, EB, E]) for n in ("wq_sb", "wk_sb", "wv_sb", "wo_sb"))
        g_sb = sb("g_sb", [P, EB])
        xw_sb = sb("xw_sb", [P, 2, C])
        xb_sb = sb("xb_sb", [P, 2])
        wg_sb, wu_sb = (sb(n, [P, 2, EB, F], F32R) for n in ("wg_sb", "wu_sb"))
        wd_sb = sb("wd_sb", [P, 2, FB, E], F32R)
        ident = sb("ident", [P, P])
        ident_bf = sb("ident_bf", [P, P], BF16)
        mask = sb("mask", [P, 2, P], BF16)
        half_power = sb("half_power", [P, 8])
        lam_sb = sb("lam_sb", [P, 4, D])
        lam_w = sb("lam_w", [P, 2, D])
        lam_d = sb("lam_d", [P, 2])
        lam_e = sb("lam_e", [P, 2])
        neg_lam = sb("neg_lam", [P, 1])
        x_tok = sb("x_tok", [P, TB, E])
        x_tr = sb("x_tr", [P, 2, EB, T])
        ctx_tr = sb("ctx_tr", [P, T])
        qk = sb("qk", [P, 2, 2, T])
        q_part = sb("q_part", [P, PARTS, 2, T], BF16)
        k_part = sb("k_part", [P, PARTS, 2, T], BF16)
        q_stacks = [sb(f"q_stack{i}", [P, N2, T], BF16) for i in range(2)]
        k_stacks = [sb(f"k_stack{i}", [P, N2, T], BF16) for i in range(2)]
        v_sb = sb("v_sb", [P, 3, TB, H, 32])
        nmax3 = sb("nmax3", [P, N2, 3])
        nmax = sb("nmax", [P, TB, N2])
        m_part = sb("m_part", [P, TB, PARTS, N2], BF16)
        mT = sb("mT", [PARTS * N2, T], BF16)
        prob = sb("prob", [P, RING, 2, 384])
        oT = sb("oT", [P, 2, 512])
        rsum = sb("rsum", [P, 2, 8])
        a_map = sb("a_map", [P, 2, 8 * DV])
        o_q = sb("o_q", [P, 2, 2, 4 * DV])
        ss = sb("ss", [P, 2, 8])
        ms = sb("ms", [P, 2, 8])
        rms = sb("rms", [P, 2, 8])
        o_tok = sb("o_tok", [P, TB, E])
        qkx = sb("qkx", [P, 2, T])
        neg_emax = sb("neg_emax", [P, TB])
        esum = sb("esum", [P, TB])
        erec = sb("erec", [P, TB])
        e_sb = sb("e_sb", [P, TB, T])
        attn_xT = sb("attn_xT", [P, TB, T])
        z = sb("z", [P, TB, E])
        stats = sb("stats", [P, TB, 6])
        mv = sb("mv", [P, TB, 2])
        var_eps = sb("var_eps", [P, TB])
        rstd = sb("rstd", [P, TB])
        x1 = z
        x2, x3 = (sb(n, [P, TB, E]) for n in ("x2", "x3"))
        x1T = sb("x1T", [P, EB, T])
        o_tr = x1T
        x2T = sb("x2T", [P, 2, EB, T], F32R)
        th = sb("th", [P, 2, T])
        hT = sb("hT", [P, 2, HELD, T], F32R)

        score = [ctx.enter_context(nc.psum_tensor(f"score{i}", [P, 1024], F32)) for i in range(2)]
        x_score, s_score = score
        pv_bank = ctx.enter_context(nc.psum_tensor("pv_bank", [P, 512], F32))
        ta, tb, tc = (ctx.enter_context(nc.psum_tensor(f"t{i}", [P, 512], F32)) for i in "abc")

        names_in = "x_tr0 x_tr1 x_tok ctx_tr wq wk wv wo lam g xw xb wg wu wd".split()
        loaded = {n: sem(f"in_{n}") for n in names_in}
        stack_in = [sem(f"stack_in{i}") for i in range(2)]
        m_rows_in = sem("m_rows_in")
        stored = sem("stored")
        q_zeros, k_ones, v_ones = sem("q_zeros"), sem("k_ones"), sem("v_ones")
        v_zeros, th_zeros = sem("v_zeros"), sem("th_zeros")
        raw_const, ident_made, mask_made, ident_bf_made = sem("raw_const"), sem("ident_made"), sem("mask_made"), sem("ident_bf_made")
        wog_made, lam_dots, lam_exp = sem("wog_made"), sem("lam_dots"), sem("lam_exp")
        q_proj, k_proj, v_proj = sem("q_proj"), sem("k_proj"), sem("v_proj")
        q_out, k_out, v_out = sem("q_out"), sem("k_out"), sem("v_out")
        q_clamped, q_parts, k_parts = sem("q_clamped"), sem("q_parts"), sem("k_parts")
        s_ready, s_max = sem("s_ready"), sem("s_max")
        m_parts, mT_ready, mT_out = sem("m_parts"), sem("mT_ready"), sem("mT_out")
        st_ready, exp_done, masked = sem("st_ready"), sem("exp_done"), sem("masked")
        pv_ready, pv_out, pvT_ready, pvT_used = sem("pv_ready"), sem("pv_out"), sem("pvT_ready"), sem("pvT_used")
        ss_ready, rms_ready, o_ready = sem("ss_ready"), sem("rms_ready"), sem("o_ready")
        qkx_ready, qkx_out = sem("qkx_ready"), sem("qkx_out")
        oT_ready, oT_out, y_ready = sem("oT_ready"), sem("oT_out"), sem("y_ready")
        e_ready, e_max, e_exp, a_ready = sem("e_ready"), sem("e_max"), sem("e_exp"), sem("a_ready")
        aT_ready, aT_out = sem("aT_ready"), sem("aT_out")
        z1_done, z2_done, z3_done = sem("z1_done"), sem("z2_done"), sem("z3_done")
        var_ready, rstd_ready = sem("var_ready"), sem("rstd_ready")
        x1_done, x2_done, x3_done = sem("x1_done"), sem("x2_done"), sem("x3_done")
        x1T_ready, x1T_out, x2T_ready, x2T_out = sem("x1T_ready"), sem("x1T_out"), sem("x2T_ready"), sem("x2T_out")
        x2T_high, w_high, w_low = sem("x2T_high"), sem("w_high"), sem("w_low")
        xm_ready = sem("xm_ready")
        hid_ready, tanh_done, h_done, h_high = sem("hid_ready"), sem("tanh_done"), sem("h_done"), sem("h_high")
        h_low, down_done = sem("h_low"), sem("down_done")
        dve_step, pool_step = sem("dve_step"), sem("pool_step")

        block = ctx.enter_context(nc.Block())

        def hidden_bank(t, j):
            return s_score[:, 512 * (j % 2):512 * (j % 2) + 512] if t >= B - 2 else tc[:]

        def pvT_bank(b, quad):
            return tb if quad < 2 else c_bank(b)

        def c_bank(b):
            return tc if b == B - 1 else ta

        def energy_bank(b):
            return tc if b == B - 1 else tb

        def raw(i):
            return prob[:].rearrange("p u m q -> p (u m q)")[:, EB * F * i:EB * F * (i + 1)].rearrange("p (e f) -> p e f", e=EB)

        def wd_rows(w, half):
            return w[:, half * FB // 2:(half + 1) * FB // 2].rearrange("p f e -> p (f e)")

        norms = [norm for b in range(1, B) for norm in ((b - 1, 0), (b - 1, 1), (b - 2, 2)) if norm[0] >= 0]
        norms += [(B - 1, 0), (B - 1, 1), (B - 2, 2), (B - 1, 2)]

        def norm_count(t, n):
            return norms.index((t, n)) + 1

        def wait_stack(eng, b):
            eng.wait_ge(stack_in[b % 2], 16 * (2 * len(PAIRS) * (b // 2 + 1) + b // 2))

        def wait(eng, s, n):
            if n > 0:
                eng.wait_ge(s, n)

        @block.sync
        def _(sp):
            def load(dst, src, name):
                sp.dma_start(dst, src).then_inc(loaded[name], 16)

            load(x_tr[:, 0], xT[0], "x_tr0")
            load(wk_sb[:], wkT, "wk")
            load(x_tr[:, 1], xT[1], "x_tr1")
            load(raw(0), wgT, "wg")
            load(raw(1), wuT, "wu")
            load(lam_sb[:], lam_in, "lam")
            load(wo_sb[:], woT, "wo")
            load(g_sb[:], g_in, "g")
            load(xw_sb[:], xwT, "xw")
            load(xb_sb[:], xb, "xb")
            load(x_tok[:], x[0], "x_tok")
            load(ctx_tr[:], ctxT[0], "ctx_tr")

            def stack(b):
                i = b % 2
                if b < 2:
                    sp.wait_ge(k_ones, b + 1)
                    sp.wait_ge(q_zeros, b + 1)
                if b >= 2:
                    sp.wait_ge(st_ready, N2 * (b - 1))
                    sp.dma_start(q_stacks[i][M_ROW:M_ROW + PARTS, :, :], q_stacks[i][M_ROW + PARTS:M_ROW + 2 * PARTS, :, :]).then_inc(stack_in[i], 16)
                for part in range(PARTS):
                    sp.wait_ge(q_parts, PARTS * b + part + 1)
                    for g, (pq, _) in enumerate(PAIRS):
                        if pq == part:
                            sp.dma_start(q_stacks[i][D * g:D * g + D, :, :], q_part[:, pq]).then_inc(stack_in[i], 16)
                    sp.wait_ge(k_parts, PARTS * b + part + 1)
                    for g, (_, pk) in enumerate(PAIRS):
                        if pk == part:
                            sp.dma_start(k_stacks[i][D * g:D * g + D, :, :], k_part[:, pk]).then_inc(stack_in[i], 16)

            def store(t):
                sp.wait_ge(x3_done, t + 1)
                sp.dma_start(out[t], x3[:]).then_inc(stored, 16)

            stack(0)
            stack(1)
            sp.wait_ge(v_proj, 1)
            load(x_tr[:, 0], xT[2], "x_tr0")
            sp.wait_ge(w_low, EB)
            load(raw(0), wdT.rearrange("p f e -> p (f e)").rearrange("p (a b) -> p a b", a=EB), "wd")
            for b in range(B):
                if b >= 2:
                    store(b - 2)
                if b > 0:
                    sp.wait_ge(z1_done, b)
                    load(x_tok[:], x[b], "x_tok")
                if b + 3 < B:
                    sp.wait_ge(v_proj, b + 2)
                    load(x_tr[:, (b + 3) % 2], xT[b + 3], f"x_tr{(b + 3) % 2}")
                if b + 2 < B:
                    stack(b + 2)
                if b + 1 < B:
                    sp.wait_ge(qkx_ready, b + 1)
                    load(ctx_tr[:], ctxT[b + 1], "ctx_tr")
            store(B - 2)
            store(B - 1)
            sp.wait_ge(stored, 16 * B)

        @block.gpsimd
        def _(pool):
            step = [0]

            def link(ins):
                step[0] += 1
                ins.then_inc(pool_step, 1)
                pool.wait_ge(pool_step, step[0])

            def ones_in_k(i):
                nc.gpsimd.memset(k_stacks[i][:].bitcast(U32), 0x3F803F80).then_inc(k_ones, 1)

            nc.gpsimd.memset(th[:], 0.0).then_inc(th_zeros, 1)
            nc.gpsimd.memset(ident[:], 0.0).then_inc(raw_const, 1)
            nc.gpsimd.memset(mask[:], 0.0).then_inc(raw_const, 1)
            ones_in_k(0)
            nc.gpsimd.memset(half_power[:], -0.5).then_inc(raw_const, 1)
            pool.wait_ge(raw_const, 3)
            nc.gpsimd.affine_select(out=ident[:], in_=ident[:], compare_op=ALU.not_equal, fill=1.0, base=0,
                                    pattern=[[-1, P]], channel_multiplier=1).then_inc(ident_made, 1)
            nc.gpsimd.affine_select(out=mask[:], in_=mask[:], compare_op=ALU.is_ge, fill=MASKED, base=0,
                                    pattern=[[0, 2], [-1, P]], channel_multiplier=1).then_inc(mask_made, 1)

            def q_split_0(b):
                pool.wait_ge(q_clamped, b + 1)
                if b > 0:
                    wait_stack(pool, b - 1)
                q, part = qk[:, 0], q_part
                nc.gpsimd.tensor_scalar(part[:, 0], q, 1.0, 0.0, ALU.mult, ALU.add).then_inc(q_parts, 1)
                pool.wait_ge(q_parts, PARTS * b + 1)
                link(nc.gpsimd.tensor_tensor(q, q, part[:, 0], ALU.subtract))

            def q_split_1(b):
                q, part = qk[:, 0], q_part
                nc.gpsimd.tensor_scalar(part[:, 1], q, 1.0, 0.0, ALU.mult, ALU.add).then_inc(q_parts, 1)
                pool.wait_ge(q_parts, PARTS * b + 2)
                link(nc.gpsimd.tensor_tensor(q, q, part[:, 1], ALU.subtract))

            def q_split_2(b):
                nc.gpsimd.tensor_scalar(q_part[:, 2], qk[:, 0], 1.0, 0.0, ALU.mult, ALU.add).then_inc(q_parts, 1)

            def q_split(b):
                q_split_0(b)
                q_split_1(b)
                q_split_2(b)

            def layer_rstd(t, n):
                pool.wait_ge(var_ready, norm_count(t, n))
                link(nc.gpsimd.tensor_scalar(var_eps[:], mv[:, :, 1], 1.0, EPS, ALU.mult, ALU.add))
                nc.gpsimd.tensor_tensor(rstd[:], var_eps[:], half_power[:, 0:TB], ALU.pow).then_inc(rstd_ready, 1)

            def causal(b, u):
                pool.wait_ge(exp_done, N2 * b + 2 * (u + 1))
                p = prob[:, (H * b + u) % RING]
                for col in (0, T):
                    ins = nc.gpsimd.affine_select(out=p[:, :, col:col + P], in_=p[:, :, col:col + P], compare_op=ALU.is_ge,
                                                  fill=0.0, base=0, pattern=[[0, 2], [1, P]], channel_multiplier=-1)
                ins.then_inc(masked, 1)

            def hidden_low(t, j):
                pool.wait_ge(h_high, FB * t + j + 1)
                nc.gpsimd.tensor_tensor(hT[:, 1, j % HELD], th[:, j % 2], hT[:, 0, j % HELD], ALU.subtract).then_inc(h_low, 1)

            def head_rms(b, quad):
                pool.wait_ge(ss_ready, QUADS * b + quad + 1)
                s = quad % 2
                link(nc.gpsimd.tensor_scalar(ms[:, s], ss[:, s], 1.0 / DV, EPS, ALU.mult, ALU.add))
                nc.gpsimd.tensor_tensor(rms[:, s], ms[:, s], half_power[:], ALU.pow).then_inc(rms_ready, 1)

            def first_body():
                causal(0, 0)
                causal(0, 1)
                causal(0, 2)
                causal(0, 3)
                causal(0, 4)
                causal(0, 5)
                causal(0, 6)
                q_split_0(2)
                causal(0, 7)
                causal(0, 8)
                q_split_1(2)
                causal(0, 9)
                causal(0, 10)
                causal(0, 11)
                head_rms(0, 0)
                head_rms(0, 1)
                q_split_2(2)
                causal(0, 12)
                causal(0, 13)
                causal(0, 14)
                causal(0, 15)
                head_rms(0, 2)
                head_rms(0, 3)

            def second_body():
                b, t = 1, 0
                causal(b, 0)
                causal(b, 1)
                causal(b, 2)
                causal(b, 3)
                causal(b, 4)
                layer_rstd(t, 0)
                causal(b, 5)
                causal(b, 6)
                causal(b, 7)
                layer_rstd(t, 1)
                causal(b, 8)
                q_split_0(b + 2)
                causal(b, 9)
                causal(b, 10)
                head_rms(b, 0)
                hidden_low(t, 0)
                q_split_1(b + 2)
                causal(b, 11)
                hidden_low(t, 1)
                q_split_2(b + 2)
                causal(b, 12)
                hidden_low(t, 2)
                hidden_low(t, 3)
                hidden_low(t, 4)
                causal(b, 13)
                head_rms(b, 1)
                causal(b, 14)
                causal(b, 15)
                head_rms(b, 2)
                hidden_low(t, 5)
                hidden_low(t, 6)
                hidden_low(t, 7)
                head_rms(b, 3)

            def third_body():
                b, t = 2, 1
                causal(b, 0)
                causal(b, 1)
                causal(b, 2)
                causal(b, 3)
                causal(b, 4)
                layer_rstd(t, 0)
                causal(b, 5)
                causal(b, 6)
                causal(b, 7)
                layer_rstd(t, 1)
                layer_rstd(t - 1, 2)
                causal(b, 8)
                causal(b, 9)
                causal(b, 10)
                head_rms(b, 0)
                causal(b, 11)
                hidden_low(t, 0)
                hidden_low(t, 1)
                causal(b, 12)
                hidden_low(t, 2)
                hidden_low(t, 3)
                head_rms(b, 1)
                causal(b, 13)
                hidden_low(t, 4)
                causal(b, 14)
                causal(b, 15)
                head_rms(b, 2)
                hidden_low(t, 5)
                hidden_low(t, 6)
                hidden_low(t, 7)
                head_rms(b, 3)

            def last_body():
                b, t = B - 1, B - 2
                causal(b, 0)
                causal(b, 1)
                causal(b, 2)
                causal(b, 3)
                layer_rstd(t, 0)
                causal(b, 4)
                causal(b, 5)
                causal(b, 6)
                layer_rstd(t, 1)
                causal(b, 7)
                causal(b, 8)
                causal(b, 9)
                layer_rstd(t - 1, 2)
                causal(b, 10)
                causal(b, 11)
                hidden_low(t, 0)
                hidden_low(t, 1)
                causal(b, 12)
                causal(b, 13)
                head_rms(b, 0)
                head_rms(b, 1)
                causal(b, 14)
                hidden_low(t, 2)
                causal(b, 15)
                hidden_low(t, 3)
                hidden_low(t, 4)
                head_rms(b, 2)
                head_rms(b, 3)
                hidden_low(t, 5)
                layer_rstd(b, 0)
                hidden_low(t, 6)
                hidden_low(t, 7)
                layer_rstd(b, 1)
                layer_rstd(t, 2)
                for j in range(FB):
                    hidden_low(b, j)
                layer_rstd(b, 2)

            nc.gpsimd.memset(v_sb[:], 0.0).then_inc(v_zeros, 1)
            q_split(0)
            ones_in_k(1)
            q_split(1)
            for i, w in enumerate((wg_sb, wu_sb)):
                for e in range(EB):
                    pool.wait_ge(w_high, EB * i + e + 1)
                    nc.gpsimd.tensor_tensor(w[:, 1, e], raw(i)[:, e], w[:, 0, e], ALU.subtract).then_inc(w_low, 1)
            for half in range(2):
                pool.wait_ge(w_high, 2 * EB + half + 1)
                nc.gpsimd.tensor_tensor(wd_rows(wd_sb[:, 1], half), raw(0)[:, half], wd_rows(wd_sb[:, 0], half),
                                        ALU.subtract).then_inc(w_low, 1)
            first_body()
            second_body()
            third_body()
            last_body()

        @block.scalar
        def _(act):
            def load(dst, src, name):
                act.dma_start(dst, src).then_inc(loaded[name], 16)

            load(wq_sb[:], wqT, "wq")
            load(wv_sb[:], wvT, "wv")

            def flat(t):
                return t.rearrange("p a b -> p (a b)")

            def q_copy(b, bank):
                act.wait_ge(q_proj, b + 1)
                wait(act, q_parts, PARTS * b)
                nc.scalar.activation(flat(qk[:, 0]), bank, ACT.Copy, scale=SCALING).then_inc(q_out, 1)

            def k_copy(b, bank):
                act.wait_ge(k_proj, b + 1)
                wait(act, k_parts, PARTS * b)
                nc.scalar.activation(flat(qk[:, 1]), bank, ACT.Copy).then_inc(k_out, 1)

            def v_copy(b, bank):
                act.wait_ge(v_proj, b + 1)
                wait(act, pv_ready, QUADS * (b - 2))
                nc.scalar.activation(v_sb[:, b % 3, :, :, 0:DV], bank.rearrange("p (a h d) -> p a h d", a=TB, h=H),
                                     ACT.Copy).then_inc(v_out, 1)

            def qkx_copy(t):
                act.wait_ge(qkx_ready, t + 1)
                if t == 0:
                    act.wait_ge(loaded["xb"], 16)
                for i in range(2):
                    nc.scalar.activation(qkx[:, i], c_bank(t)[:, T * i:T * i + T], ACT.Identity,
                                         bias=xb_sb[:, i:i + 1]).then_inc(qkx_out, 1)

            def copy_out(t, dst, bank, ready, done):
                act.wait_ge(ready, t + 1)
                nc.scalar.activation(flat(dst[:]), bank[:], ACT.Copy).then_inc(done, 1)

            def x2T_copy(t):
                act.wait_ge(x2T_ready, t + 1)
                nc.scalar.activation(flat(x2T[:, 0]), ta[:], ACT.Copy).then_inc(x2T_high, 1)

            def energy_exp(t):
                act.wait_ge(e_max, t + 1)
                for i in range(TB):
                    nc.scalar.activation(e_sb[:, i], energy_bank(t)[:, T * i:T * i + T], ACT.Exp, bias=neg_emax[:, i:i + 1],
                                         accum_out=esum[:, i:i + 1]).then_inc(e_exp, 1)

            def tanh_gate(t, j):
                act.wait_ge(hid_ready, FB * t + j + 1)
                wait(act, h_low, FB * t + j - 1)
                nc.scalar.activation(th[:, j % 2], hidden_bank(t, j)[:, 0:T], ACT.Tanh, scale=0.5).then_inc(tanh_done, 1)

            def hidden_high(t, j):
                act.wait_ge(h_done, FB * t + j + 1)
                wait(act, down_done, FB * t + j + 1 - HELD)
                nc.scalar.activation(hT[:, 0, j % HELD], th[:, j % 2], ACT.Copy).then_inc(h_high, 1)

            def m_out(b):
                act.wait_ge(mT_ready, b + 1)
                wait(act, m_rows_in, 16 * b)
                nc.scalar.activation(mT[:], pv_bank[0:PARTS * N2, 0:T // 2].bitcast(BF16), ACT.Copy).then_inc(mT_out, 1)
                act.wait_ge(mT_out, b + 1)
                wait_stack(act, b)
                act.dma_start(q_stacks[b % 2][M_ROW:M_ROW + PARTS, :, :], mT[:]).then_inc(m_rows_in, 16)

            def prob_exp(b, u):
                if H * b + u >= RING:
                    act.wait_ge(pv_ready, (H * b + u - RING) // 4 + 1)
                if b == 0 and u == 0:
                    act.wait_ge(w_low, 2 * EB + 2)
                for m in range(2):
                    act.wait_ge(st_ready, N2 * b + 2 * u + m + 1)
                    nc.scalar.activation(prob[:, (H * b + u) % RING, m], x_score[:, 512 * m:512 * m + 384], ACT.Exp).then_inc(exp_done, 1)

            def pv_copy(b, quad):
                act.wait_ge(pv_ready, QUADS * b + quad + 1)
                wait(act, pvT_ready, QUADS * b + quad - 1)
                nc.scalar.activation(oT[:, quad % 2], pv_bank[:], ACT.Copy).then_inc(pv_out, 1)

            def first_body():
                prob_exp(0, 0)
                prob_exp(0, 1)
                prob_exp(0, 2)
                prob_exp(0, 3)
                prob_exp(0, 4)
                q_copy(2, tb[:])
                prob_exp(0, 5)
                pv_copy(0, 0)
                prob_exp(0, 6)
                k_copy(2, tc[:])
                prob_exp(0, 7)
                v_copy(2, tc[:])
                prob_exp(0, 8)
                prob_exp(0, 9)
                pv_copy(0, 1)
                prob_exp(0, 10)
                prob_exp(0, 11)
                qkx_copy(0)
                prob_exp(0, 12)
                pv_copy(0, 2)
                prob_exp(0, 13)
                prob_exp(0, 14)
                energy_exp(0)
                prob_exp(0, 15)
                copy_out(0, attn_xT, ta, aT_ready, aT_out)
                m_out(1)
                pv_copy(0, 3)

            def second_body():
                b, t = 1, 0
                prob_exp(b, 0)
                prob_exp(b, 1)
                prob_exp(b, 2)
                copy_out(t, o_tr, ta, oT_ready, oT_out)
                prob_exp(b, 3)
                prob_exp(b, 4)
                prob_exp(b, 5)
                pv_copy(b, 0)
                q_copy(b + 2, tb[:])
                copy_out(t, x1T, ta, x1T_ready, x1T_out)
                prob_exp(b, 6)
                prob_exp(b, 7)
                k_copy(b + 2, tc[:])
                v_copy(b + 2, tc[:])
                x2T_copy(t)
                prob_exp(b, 8)
                prob_exp(b, 9)
                prob_exp(b, 10)
                pv_copy(b, 1)
                tanh_gate(t, 0)
                hidden_high(t, 0)
                tanh_gate(t, 1)
                prob_exp(b, 11)
                hidden_high(t, 1)
                tanh_gate(t, 2)
                prob_exp(b, 12)
                qkx_copy(b)
                pv_copy(b, 2)
                hidden_high(t, 2)
                tanh_gate(t, 3)
                energy_exp(b)
                tanh_gate(t, 4)
                hidden_high(t, 3)
                hidden_high(t, 4)
                prob_exp(b, 13)
                tanh_gate(t, 5)
                prob_exp(b, 14)
                prob_exp(b, 15)
                copy_out(b, attn_xT, ta, aT_ready, aT_out)
                tanh_gate(t, 6)
                hidden_high(t, 5)
                pv_copy(b, 3)
                m_out(b + 1)
                tanh_gate(t, 7)
                hidden_high(t, 6)
                hidden_high(t, 7)

            def third_body():
                b, t = 2, 1
                prob_exp(b, 0)
                prob_exp(b, 1)
                prob_exp(b, 2)
                copy_out(t, o_tr, ta, oT_ready, oT_out)
                prob_exp(b, 3)
                prob_exp(b, 4)
                pv_copy(b, 0)
                prob_exp(b, 5)
                copy_out(t, x1T, ta, x1T_ready, x1T_out)
                prob_exp(b, 6)
                prob_exp(b, 7)
                pv_copy(b, 1)
                x2T_copy(t)
                prob_exp(b, 8)
                prob_exp(b, 9)
                prob_exp(b, 10)
                tanh_gate(t, 0)
                hidden_high(t, 0)
                prob_exp(b, 11)
                tanh_gate(t, 1)
                qkx_copy(b)
                hidden_high(t, 1)
                tanh_gate(t, 2)
                prob_exp(b, 12)
                pv_copy(b, 2)
                hidden_high(t, 2)
                tanh_gate(t, 3)
                energy_exp(b)
                hidden_high(t, 3)
                tanh_gate(t, 4)
                hidden_high(t, 4)
                prob_exp(b, 13)
                tanh_gate(t, 5)
                prob_exp(b, 14)
                hidden_high(t, 5)
                prob_exp(b, 15)
                tanh_gate(t, 6)
                copy_out(b, attn_xT, ta, aT_ready, aT_out)
                pv_copy(b, 3)
                m_out(b + 1)
                tanh_gate(t, 7)
                hidden_high(t, 6)
                hidden_high(t, 7)

            def last_body():
                b, t = B - 1, B - 2
                prob_exp(b, 0)
                prob_exp(b, 1)
                copy_out(t, o_tr, ta, oT_ready, oT_out)
                prob_exp(b, 2)
                prob_exp(b, 3)
                prob_exp(b, 4)
                qkx_copy(b)
                copy_out(t, x1T, ta, x1T_ready, x1T_out)
                pv_copy(b, 0)
                prob_exp(b, 5)
                energy_exp(b)
                prob_exp(b, 6)
                prob_exp(b, 7)
                copy_out(b, attn_xT, tc, aT_ready, aT_out)
                prob_exp(b, 8)
                prob_exp(b, 9)
                x2T_copy(t)
                prob_exp(b, 10)
                pv_copy(b, 1)
                tanh_gate(t, 0)
                tanh_gate(t, 1)
                prob_exp(b, 11)
                hidden_high(t, 0)
                prob_exp(b, 12)
                hidden_high(t, 1)
                prob_exp(b, 13)
                pv_copy(b, 2)
                tanh_gate(t, 2)
                tanh_gate(t, 3)
                prob_exp(b, 14)
                hidden_high(t, 2)
                prob_exp(b, 15)
                tanh_gate(t, 4)
                hidden_high(t, 3)
                hidden_high(t, 4)
                pv_copy(b, 3)
                tanh_gate(t, 5)
                tanh_gate(t, 6)
                copy_out(b, o_tr, ta, oT_ready, oT_out)
                hidden_high(t, 5)
                copy_out(b, x1T, ta, x1T_ready, x1T_out)
                tanh_gate(t, 7)
                hidden_high(t, 6)
                hidden_high(t, 7)
                x2T_copy(b)
                for j in range(FB):
                    tanh_gate(b, j)
                    if j > 0:
                        hidden_high(b, j - 1)
                hidden_high(b, FB - 1)

            q_copy(0, ta[:])
            k_copy(0, tb[:])
            act.wait_ge(v_ones, 1)
            v_copy(0, tc[:])
            q_copy(1, x_score[:, 0:512])
            k_copy(1, x_score[:, 512:1024])
            v_copy(1, s_score[:, 0:512])
            for i, (w, name) in enumerate(((wg_sb, "wg"), (wu_sb, "wu"))):
                act.wait_ge(loaded[name], 16)
                for e in range(EB):
                    nc.scalar.activation(w[:, 0, e], raw(i)[:, e], ACT.Copy).then_inc(w_high, 1)
            act.wait_ge(lam_dots, 1)
            nc.scalar.activation(lam_e[:], lam_d[:], ACT.Exp).then_inc(lam_exp, 1)
            act.wait_ge(loaded["wd"], 16)
            for half in range(2):
                nc.scalar.activation(wd_rows(wd_sb[:, 0], half), raw(0)[:, half], ACT.Copy).then_inc(w_high, 1)
            m_out(0)
            first_body()
            second_body()
            third_body()
            last_body()

        @block.tensor
        def _(pe):
            def matmuls(out_ap, pairs):
                for n, (lhsT, rhs) in enumerate(pairs):
                    mm = nc.tensor.matmul(out_ap, lhsT, rhs, start=(n == 0), stop=(n == len(pairs) - 1))
                return mm

            def blk(i):
                return slice(P * i, P * i + P)

            def project_qk(b, bank, w, done):
                pe.wait_ge(loaded[f"x_tr{b % 2}"], 16 * (b // 2 + 1))
                for half in range(2):
                    mm = matmuls(bank[:, T * half:T * half + T],
                                 [(w[:, e, blk(half)], x_tr[:, b % 2, e, :]) for e in range(EB)])
                mm.then_inc(done, 1)

            def project_v(b, bank):
                for i in range(TB):
                    mm = matmuls(bank[:, E * i:E * i + E], [(x_tr[:, b % 2, e, blk(i)], wv_sb[:, e, :]) for e in range(EB)])
                mm.then_inc(v_proj, 1)

            def four_transposes(bank, src):
                for i in range(2):
                    for j in range(2):
                        mm = nc.tensor.transpose(bank[:, T * j + P * i:T * j + P * i + P], src[:, i, blk(j)], ident[:])
                return mm

            def heads_transposed(t):
                pe.wait_ge(o_ready, QUADS * (t + 1))
                pe.wait_ge(pvT_used, QUADS * (t + 1))
                if t == B - 1:
                    pe.wait_ge(x2T_out, t)
                four_transposes(ta, o_tok).then_inc(oT_ready, 1)

            def project_out(t):
                pe.wait_ge(oT_out, t + 1)
                if t == 0:
                    pe.wait_ge(wog_made, 2)
                for i in range(TB):
                    mm = matmuls(ta[:, E * i:E * i + E], [(o_tr[:, e, blk(i)], wo_sb[:, e, :]) for e in range(EB)])
                mm.then_inc(y_ready, 1)

            def x1_transposed(t):
                pe.wait_ge(x1_done, t + 1)
                four_transposes(ta, x1).then_inc(x1T_ready, 1)

            def cross(t):
                pe.wait_ge(x1T_out, t + 1)
                pe.wait_ge(aT_out, t + 1)
                for i in range(TB):
                    mm = matmuls(ta[:, T * i:T * i + T], [(x1T[:, n, blk(i)], attn_xT[:, n, :]) for n in range(TB)])
                mm.then_inc(xm_ready, 1)

            def x2_transposed(t):
                pe.wait_ge(x2_done, t + 1)
                four_transposes(ta, x2).then_inc(x2T_ready, 1)

            def cross_qk(b):
                pe.wait_ge(loaded["ctx_tr"], 16 * (b + 1))
                if b == 0:
                    pe.wait_ge(loaded["xw"], 16)
                if b == B - 1:
                    pe.wait_ge(h_done, FB * (b - 1))
                else:
                    wait(pe, x2T_out, b)
                for i in range(2):
                    mm = nc.tensor.matmul(c_bank(b)[:, T * i:T * i + T], xw_sb[:, i, :], ctx_tr[:], start=True, stop=True)
                mm.then_inc(qkx_ready, 1)

            def energy(b):
                pe.wait_ge(qkx_out, 2 * (b + 1))
                if b < B - 1:
                    pe.wait_ge(pvT_used, QUADS * b + 2)
                for i in range(TB):
                    mm = nc.tensor.matmul(energy_bank(b)[:, T * i:T * i + T], qkx[:, 0, blk(i)], qkx[:, 1, :], start=True, stop=True)
                mm.then_inc(e_ready, 1)

            def cross_transposed(b):
                pe.wait_ge(a_ready, b + 1)
                if b < B - 1:
                    pe.wait_ge(pvT_used, QUADS * b + 3)
                four_transposes(c_bank(b), e_sb).then_inc(aT_ready, 1)

            def hidden(t, j):
                bank = hidden_bank(t, j)
                if j == 0:
                    pe.wait_ge(x2T_out, t + 1)
                    if t == 0:
                        pe.wait_ge(w_low, 2 * EB)
                if t >= B - 2:
                    pe.wait_ge(s_max, N2 * B)
                    pe.wait_ge(h_done, FB * t + j - 1)
                elif j == 0:
                    pe.wait_ge(v_out, min(t + 4, B))
                    wait(pe, h_done, FB * t)
                else:
                    pe.wait_ge(h_done, FB * t + j)
                for n, w in enumerate((wg_sb, wu_sb)):
                    mm = matmuls(bank[:, T * n:T * n + T], [(w[:, wp, e, blk(j)], x2T[:, xp, e, :]) for e in range(EB)
                                                            for wp, xp in ((0, 0), (0, 1), (1, 0))])
                mm.then_inc(hid_ready, 1)

            def down(t, j):
                pe.wait_ge(h_low, FB * t + j + 1)
                if t == 0 and j == 0:
                    pe.wait_ge(w_low, 2 * EB + 2)
                if j == 0 and t < B - 2:
                    pe.wait_ge(e_exp, TB * (t + 2))
                elif j == 0 and t == B - 2:
                    pe.wait_ge(pvT_used, QUADS * (t + 1) + 2)
                elif j == 0:
                    pe.wait_ge(z3_done, t)
                for i in range(TB):
                    for hp, wp in ((0, 0), (0, 1), (1, 0)):
                        first, last = j == 0 and i == 0 and hp == wp, j == FB - 1 and hp == 1
                        mm = nc.tensor.matmul(tb[:, E * i:E * i + E], hT[:, hp, j % HELD, blk(i)], wd_sb[:, wp, j, :],
                                              start=first, stop=last, skip_group_check=True)
                mm.then_inc(down_done, 1)

            def scores(b, u, s):
                if u == 0:
                    wait_stack(pe, b)
                    if b == 0:
                        pe.wait_ge(q_out, 2)
                        pe.wait_ge(k_out, 2)
                        pe.wait_ge(v_out, 2)
                        pe.wait_ge(ident_bf_made, 1)
                        pe.wait_ge(mask_made, 1)
                q_stack, k_stack = q_stacks[b % 2], k_stacks[b % 2]
                for m in range(2):
                    n = 2 * u + m
                    if b == 0:
                        wait(pe, s_max, n - 3)
                    else:
                        pe.wait_ge(s_max, N2 * b + n - 1)
                    bank = s[:, 512 * m:512 * m + 384]
                    nc.tensor.matmul(bank[:, 0:P], q_stack[:, n, blk(0)], k_stack[:, n, blk(0)],
                                     start=True, stop=False, skip_group_check=True)
                    nc.tensor.matmul(bank[:, P:3 * P], q_stack[:, n, blk(1)], k_stack[:, n, :],
                                     start=False, stop=False, skip_group_check=True)
                    diagonal = bank.rearrange("p (a k) -> p a k", a=3)[:, 0:3:2, :]
                    nc.tensor.matmul(diagonal, ident_bf[:], mask[:],
                                     start=False, stop=True, skip_group_check=True).then_inc(s_ready, 1)

            def maxima_transposed(b):
                pe.wait_ge(m_parts, b + 1)
                wait(pe, pv_out, QUADS * b - (1 if b == 1 else 0))
                for i in range(TB):
                    mm = nc.tensor.transpose(pv_bank[0:PARTS * N2, 64 * i:64 * i + 64].bitcast(BF16),
                                             m_part[:, i].rearrange("p a b -> p (a b)"), ident_bf[:])
                mm.then_inc(mT_ready, 1)

            def scores_transposed(b, u):
                if u == 0:
                    pe.wait_ge(m_rows_in, 16 * (b + 1))
                q_stack, k_stack = q_stacks[b % 2], k_stacks[b % 2]
                for m in range(2):
                    n = 2 * u + m
                    wait(pe, exp_done, N2 * b + n - 1)
                    bank = x_score[:, 512 * m:512 * m + 384]
                    nc.tensor.matmul(bank[:, 0:T], k_stack[:, n, blk(0)], q_stack[:, n, :],
                                     start=True, stop=False, skip_group_check=True)
                    nc.tensor.matmul(bank[:, T:T + P], k_stack[:, n, blk(1)], q_stack[:, n, blk(1)],
                                     start=False, stop=True, skip_group_check=True).then_inc(st_ready, 1)

            def times_v(b, quad):
                pe.wait_ge(masked, H * b + 4 * quad + 4)
                if quad == 0:
                    pe.wait_ge(v_out, b + 1)
                    pe.wait_ge(mT_out, b + 1)
                if b == 0 and quad == 3:
                    pe.wait_ge(mT_out, 2)
                wait(pe, pv_out, QUADS * b + quad)
                for i in range(4):
                    h = 4 * quad + i
                    nc.tensor.matmul(pv_bank[32 * i:32 * i + 32, :], v_sb[:, b % 3, 0, h, :], prob[:, (H * b + h) % RING, :, 0:T],
                                     start=True, stop=False)
                for i in range(4):
                    h = 4 * quad + i
                    late = pv_bank[32 * i:32 * i + 32, :].rearrange("p (m q) -> p m q", m=2)[:, :, P:T]
                    mm = nc.tensor.matmul(late, v_sb[:, b % 3, 1, h, :], prob[:, (H * b + h) % RING, :, T:T + P],
                                          start=False, stop=True)
                mm.then_inc(pv_ready, 1)

            def pv_transposed(b, quad):
                pe.wait_ge(pv_out, QUADS * b + quad + 1)
                if quad == 0:
                    pe.wait_ge(q_out, min(b + 3, B))
                    wait(pe, z3_done, b - 1)
                elif quad == 1:
                    pe.wait_ge(pvT_used, QUADS * b + 1)
                elif b == B - 1 and quad == 2:
                    pe.wait_ge(aT_out, b + 1)
                elif b == B - 1:
                    pe.wait_ge(pvT_used, QUADS * b + 3)
                elif quad == 2:
                    pe.wait_ge(qkx_out, 2 * (b + 1))
                else:
                    pe.wait_ge(aT_out, b + 1)
                bank = pvT_bank(b, quad)
                for i in range(4):
                    mm = nc.tensor.transpose(bank[:, blk(i)], oT[:, quad % 2, blk(i)], ident[:])
                mm.then_inc(pvT_ready, 1)

            def next_q(b):
                wait(pe, z3_done, b - 3)
                project_qk(b, tb, wq_sb, q_proj)

            def next_k(b):
                wait(pe, h_done, FB * (b - 3))
                project_qk(b, tc, wk_sb, k_proj)

            def next_v(b):
                pe.wait_ge(k_out, b + 1)
                project_v(b, tc)

            def first_body():
                scores(1, 3, s_score)
                scores_transposed(0, 0)
                scores(1, 4, s_score)
                scores_transposed(0, 1)
                scores(1, 5, s_score)
                scores_transposed(0, 2)
                scores(1, 6, s_score)
                scores_transposed(0, 3)
                scores_transposed(0, 4)
                scores(1, 7, s_score)
                scores_transposed(0, 5)
                scores(1, 8, s_score)
                next_q(2)
                scores(1, 9, s_score)
                times_v(0, 0)
                scores_transposed(0, 6)
                next_k(2)
                scores(1, 10, s_score)
                scores_transposed(0, 7)
                next_v(2)
                pv_transposed(0, 0)
                times_v(0, 1)
                scores(1, 11, s_score)
                scores_transposed(0, 8)
                scores(1, 12, s_score)
                scores_transposed(0, 9)
                scores_transposed(0, 10)
                pv_transposed(0, 1)
                scores(1, 13, s_score)
                scores_transposed(0, 11)
                cross_qk(0)
                scores_transposed(0, 12)
                scores(1, 14, s_score)
                times_v(0, 2)
                scores(1, 15, s_score)
                energy(0)
                scores_transposed(0, 13)
                pv_transposed(0, 2)
                scores_transposed(0, 14)
                scores_transposed(0, 15)
                cross_transposed(0)
                maxima_transposed(1)
                times_v(0, 3)
                pv_transposed(0, 3)

            def second_body():
                b, t = 1, 0
                scores(b + 1, 0, s_score)
                scores_transposed(b, 0)
                scores_transposed(b, 1)
                scores(b + 1, 1, s_score)
                scores_transposed(b, 2)
                heads_transposed(t)
                scores(b + 1, 2, s_score)
                scores_transposed(b, 3)
                scores(b + 1, 3, s_score)
                project_out(t)
                scores_transposed(b, 4)
                scores(b + 1, 4, s_score)
                times_v(b, 0)
                scores_transposed(b, 5)
                next_q(b + 2)
                scores(b + 1, 5, s_score)
                next_k(b + 2)
                x1_transposed(t)
                scores_transposed(b, 6)
                scores(b + 1, 6, s_score)
                pv_transposed(b, 0)
                cross(t)
                scores_transposed(b, 7)
                scores(b + 1, 7, s_score)
                next_v(b + 2)
                scores(b + 1, 8, s_score)
                x2_transposed(t)
                scores_transposed(b, 8)
                times_v(b, 1)
                scores(b + 1, 9, s_score)
                scores_transposed(b, 9)
                scores_transposed(b, 10)
                hidden(t, 0)
                scores(b + 1, 10, s_score)
                hidden(t, 1)
                scores_transposed(b, 11)
                pv_transposed(b, 1)
                cross_qk(b)
                scores(b + 1, 11, s_score)
                hidden(t, 2)
                scores_transposed(b, 12)
                times_v(b, 2)
                scores(b + 1, 12, s_score)
                energy(b)
                hidden(t, 3)
                scores_transposed(b, 13)
                scores(b + 1, 13, s_score)
                pv_transposed(b, 2)
                hidden(t, 4)
                down(t, 0)
                scores(b + 1, 14, s_score)
                hidden(t, 5)
                scores_transposed(b, 14)
                down(t, 1)
                scores_transposed(b, 15)
                scores(b + 1, 15, s_score)
                cross_transposed(b)
                down(t, 2)
                hidden(t, 6)
                times_v(b, 3)
                down(t, 3)
                maxima_transposed(b + 1)
                hidden(t, 7)
                down(t, 4)
                pv_transposed(b, 3)
                down(t, 5)
                down(t, 6)
                down(t, 7)

            def third_body():
                b, t = 2, 1
                scores_transposed(b, 0)
                scores(b + 1, 0, s_score)
                heads_transposed(t)
                scores_transposed(b, 1)
                scores(b + 1, 1, s_score)
                scores_transposed(b, 2)
                scores(b + 1, 2, s_score)
                scores_transposed(b, 3)
                scores(b + 1, 3, s_score)
                project_out(t)
                scores_transposed(b, 4)
                scores(b + 1, 4, s_score)
                times_v(b, 0)
                scores_transposed(b, 5)
                scores(b + 1, 5, s_score)
                x1_transposed(t)
                scores_transposed(b, 6)
                scores(b + 1, 6, s_score)
                pv_transposed(b, 0)
                scores_transposed(b, 7)
                scores(b + 1, 7, s_score)
                cross(t)
                scores(b + 1, 8, s_score)
                scores_transposed(b, 8)
                times_v(b, 1)
                x2_transposed(t)
                scores(b + 1, 9, s_score)
                scores_transposed(b, 9)
                scores_transposed(b, 10)
                hidden(t, 0)
                scores(b + 1, 10, s_score)
                pv_transposed(b, 1)
                scores_transposed(b, 11)
                hidden(t, 1)
                cross_qk(b)
                scores(b + 1, 11, s_score)
                scores_transposed(b, 12)
                hidden(t, 2)
                times_v(b, 2)
                scores(b + 1, 12, s_score)
                hidden(t, 3)
                energy(b)
                scores_transposed(b, 13)
                pv_transposed(b, 2)
                scores(b + 1, 13, s_score)
                hidden(t, 4)
                down(t, 0)
                hidden(t, 5)
                scores(b + 1, 14, s_score)
                scores_transposed(b, 14)
                down(t, 1)
                cross_transposed(b)
                scores_transposed(b, 15)
                hidden(t, 6)
                scores(b + 1, 15, s_score)
                down(t, 2)
                times_v(b, 3)
                down(t, 3)
                maxima_transposed(b + 1)
                hidden(t, 7)
                down(t, 4)
                pv_transposed(b, 3)
                down(t, 5)
                down(t, 6)
                down(t, 7)

            def last_body():
                b, t = B - 1, B - 2
                scores_transposed(b, 0)
                scores_transposed(b, 1)
                heads_transposed(t)
                scores_transposed(b, 2)
                project_out(t)
                scores_transposed(b, 3)
                scores_transposed(b, 4)
                cross_qk(b)
                scores_transposed(b, 5)
                x1_transposed(t)
                times_v(b, 0)
                energy(b)
                scores_transposed(b, 6)
                cross(t)
                scores_transposed(b, 7)
                cross_transposed(b)
                scores_transposed(b, 8)
                pv_transposed(b, 0)
                scores_transposed(b, 9)
                x2_transposed(t)
                times_v(b, 1)
                scores_transposed(b, 10)
                hidden(t, 0)
                hidden(t, 1)
                scores_transposed(b, 11)
                pv_transposed(b, 1)
                scores_transposed(b, 12)
                hidden(t, 2)
                scores_transposed(b, 13)
                times_v(b, 2)
                hidden(t, 3)
                pv_transposed(b, 2)
                scores_transposed(b, 14)
                scores_transposed(b, 15)
                hidden(t, 4)
                down(t, 0)
                times_v(b, 3)
                pv_transposed(b, 3)
                down(t, 1)
                hidden(t, 5)
                down(t, 2)
                heads_transposed(b)
                hidden(t, 6)
                project_out(b)
                hidden(t, 7)
                down(t, 3)
                down(t, 4)
                down(t, 5)
                x1_transposed(b)
                cross(b)
                down(t, 6)
                down(t, 7)
                x2_transposed(b)
                for j in range(FB):
                    hidden(b, j)
                    if j > 1:
                        down(b, j - 2)
                down(b, FB - 2)
                down(b, FB - 1)

            pe.wait_ge(th_zeros, 1)
            for i in range(WARM_UP):
                nc.tensor.matmul(pv_bank[:, 0:T], th[:, 0, blk(0)], th[:, 1, :], start=True, stop=True)

            for b, (q_bank, k_bank, v_bank) in enumerate((
                    (ta, tb, tc), (x_score[:, 0:512], x_score[:, 512:1024], s_score[:, 0:512]))):
                pe.wait_ge(loaded["wq"], 16)
                project_qk(b, q_bank, wq_sb, q_proj)
                pe.wait_ge(loaded["wk"], 16)
                project_qk(b, k_bank, wk_sb, k_proj)
                pe.wait_ge(loaded["wv"], 16)
                project_v(b, v_bank)
            for u in range(H):
                scores(0, u, score[u % 2])
            scores(1, 0, s_score)
            maxima_transposed(0)
            for u in range(1, EARLY):
                scores(1, u, s_score)
            first_body()
            second_body()
            third_body()
            last_body()

        @block.vector
        def _(dve):
            step = [0]

            def link(ins):
                step[0] += 1
                ins.then_inc(dve_step, 1)
                dve.wait_ge(dve_step, step[0])

            def zeros_in_q(i):
                nc.vector.memset(q_stacks[i][:].bitcast(U32), 0).then_inc(q_zeros, 1)

            def clamp_q(b):
                dve.wait_ge(q_out, b + 1)
                nc.vector.tensor_scalar(qk[:, 0], qk[:, 0], -LIMIT, LIMIT, ALU.max, ALU.min).then_inc(q_clamped, 1)

            def split_k_0(b):
                dve.wait_ge(k_out, b + 1)
                k, part = qk[:, 1], k_part
                link(nc.vector.tensor_scalar(k, k, -LIMIT, LIMIT, ALU.max, ALU.min))
                if b > 0:
                    wait_stack(dve, b - 1)
                nc.vector.tensor_copy(part[:, 0], k).then_inc(k_parts, 1)
                dve.wait_ge(k_parts, PARTS * b + 1)
                link(nc.vector.tensor_tensor(k, k, part[:, 0], ALU.subtract))

            def split_k_1(b):
                k, part = qk[:, 1], k_part
                nc.vector.tensor_copy(part[:, 1], k).then_inc(k_parts, 1)
                dve.wait_ge(k_parts, PARTS * b + 2)
                link(nc.vector.tensor_tensor(k, k, part[:, 1], ALU.subtract))
                nc.vector.tensor_copy(part[:, 2], k).then_inc(k_parts, 1)

            def split_k(b):
                split_k_0(b)
                split_k_1(b)

            def score_max(b, u, s):
                for m in range(2):
                    n = 2 * u + m
                    dve.wait_ge(s_ready, N2 * b + n + 1)
                    nc.vector.tensor_reduce(nmax3[:, n, :], s[:, 512 * m:512 * m + 384].rearrange("p (a k) -> p a k", k=P),
                                            AX.X, ALU.max, negate=True).then_inc(s_max, 1)

            def split_maxima(b):
                dve.wait_ge(s_max, N2 * (b + 1))
                wait(dve, mT_ready, b)
                nc.vector.tensor_copy(nmax[:, 0, :], nmax3[:, :, 0])
                link(nc.vector.tensor_tensor(nmax[:, 1, :], nmax3[:, :, 1], nmax3[:, :, 2], ALU.min))
                link(nc.vector.tensor_copy(m_part[:, :, 0], nmax[:]))
                link(nc.vector.tensor_tensor(nmax[:], nmax[:], m_part[:, :, 0], ALU.subtract))
                link(nc.vector.tensor_copy(m_part[:, :, 1], nmax[:]))
                link(nc.vector.tensor_tensor(nmax[:], nmax[:], m_part[:, :, 1], ALU.subtract))
                nc.vector.tensor_copy(m_part[:, :, 2], nmax[:]).then_inc(m_parts, 1)

            def combine(b, quad):
                s = quad % 2
                dve.wait_ge(pvT_ready, QUADS * b + quad + 1)
                bank = pvT_bank(b, quad)
                maps = bank[:].rearrange("p (m r c) -> p m r c", m=2, c=32)
                rs = rsum[:, 0:2, :]
                link(nc.vector.reciprocal(rs, maps[:, :, :, DV]))
                for m in range(2):
                    ins = nc.vector.tensor_tensor(a_map[:, m].rearrange("p (r c) -> p r c", c=DV), maps[:, m, :, 0:DV],
                                                  rsum[:, m, :].unsqueeze(2).to_broadcast([P, 8, DV]), ALU.mult)
                ins.then_inc(pvT_used, 1)
                dve.wait_ge(pvT_used, QUADS * b + quad + 1)
                o = o_q[:, s].rearrange("p a b -> p (a b)")
                link(nc.vector.scalar_tensor_tensor(out=o, in0=a_map[:, 1], scalar=neg_lam[:, 0:1],
                                                    in1=a_map[:, 0], op0=ALU.mult, op1=ALU.add))
                squares = a_map[:, 0]
                link(nc.vector.tensor_tensor(squares, o, o, ALU.mult))
                nc.vector.tensor_reduce(ss[:, s], squares.rearrange("p (r c) -> p r c", c=DV), AX.X, ALU.add).then_inc(ss_ready, 1)

            def normalise(b, quad):
                s = quad % 2
                dve.wait_ge(rms_ready, QUADS * b + quad + 1)
                wait(dve, oT_ready, b)
                for i in range(TB):
                    ins = nc.vector.tensor_tensor(
                        o_tok[:, i, 4 * DV * quad:4 * DV * (quad + 1)].rearrange("p (h c) -> p h c", c=DV),
                        o_q[:, s, i].rearrange("p (h c) -> p h c", c=DV),
                        rms[:, s, 4 * i:4 * i + 4].unsqueeze(2).to_broadcast([P, 4, DV]), ALU.mult)
                ins.then_inc(o_ready, 1)

            def layer_stats(z):
                for i in range(TB):
                    ins = nc.vector.bn_stats(stats[:, i], z[:, i])
                link(ins)
                for i in range(TB):
                    ins = nc.vector.bn_aggr(mv[:, i], stats[:, i])
                ins.then_inc(var_ready, 1)

            def layer_norm(t, n, z, dst, done):
                dve.wait_ge(rstd_ready, norm_count(t, n))
                for i in range(TB):
                    ins = nc.vector.tensor_scalar(dst[:, i], z[:, i], mv[:, i, 0:1], rstd[:, i:i + 1],
                                                  ALU.subtract, ALU.mult)
                ins.then_inc(done, 1)

            def flat(t):
                return t.rearrange("p a b -> p (a b)")

            def energy_max(t):
                dve.wait_ge(e_ready, t + 1)
                nc.vector.tensor_reduce(neg_emax[:], energy_bank(t)[:].rearrange("p (a k) -> p a k", a=TB), AX.X, ALU.max,
                                        negate=True).then_inc(e_max, 1)

            def cross_weights(t):
                dve.wait_ge(e_exp, TB * (t + 1))
                link(nc.vector.reciprocal(erec[:], esum[:]))
                for i in range(TB):
                    ins = nc.vector.tensor_scalar(e_sb[:, i], e_sb[:, i], erec[:, i:i + 1], None, ALU.mult)
                ins.then_inc(a_ready, 1)

            def first_residual(t):
                wait(dve, x2_done, t)
                dve.wait_ge(y_ready, t + 1)
                dve.wait_ge(loaded["x_tok"], 16 * (t + 1))
                nc.vector.tensor_tensor(flat(z[:]), ta[:], flat(x_tok[:]), ALU.add).then_inc(z1_done, 1)
                dve.wait_ge(z1_done, t + 1)
                layer_stats(z)

            def second_residual(t):
                dve.wait_ge(xm_ready, t + 1)
                nc.vector.tensor_tensor(flat(z[:]), ta[:], flat(x1[:]), ALU.add).then_inc(z2_done, 1)
                dve.wait_ge(z2_done, t + 1)
                layer_stats(z)

            def x2T_rest(t):
                dve.wait_ge(x2T_high, t + 1)
                nc.vector.tensor_tensor(flat(x2T[:, 1]), ta[:], flat(x2T[:, 0]), ALU.subtract).then_inc(x2T_out, 1)

            def gate(t, j):
                dve.wait_ge(tanh_done, FB * t + j + 1)
                bank = hidden_bank(t, j)
                link(nc.vector.scalar_tensor_tensor(out=th[:, j % 2], in0=th[:, j % 2], scalar=1.0,
                                                    in1=bank[:, 0:T], op0=ALU.add, op1=ALU.mult))
                nc.vector.tensor_tensor(th[:, j % 2], th[:, j % 2], bank[:, T:2 * T], ALU.mult).then_inc(h_done, 1)

            def third_residual(t):
                dve.wait_ge(down_done, FB * (t + 1))
                wait(dve, stored, 16 * t)
                nc.vector.scalar_tensor_tensor(out=flat(x3[:]), in0=tb[:], scalar=0.5, in1=flat(x2[:]), op0=ALU.mult,
                                               op1=ALU.add).then_inc(z3_done, 1)

            def third_stats(t):
                dve.wait_ge(z3_done, t + 1)
                layer_stats(x3)

            def result(t):
                layer_norm(t, 2, x3, x3, x3_done)

            def late_constants():
                dve.wait_ge(lam_exp, 1)
                link(nc.vector.scalar_tensor_tensor(out=neg_lam[:], in0=lam_e[:, 1:2], scalar=LAMBDA_INIT,
                                                    in1=lam_e[:, 0:1], op0=ALU.subtract, op1=ALU.subtract))
                dve.wait_ge(loaded["wo"], 16)
                dve.wait_ge(loaded["g"], 16)
                for e in range(EB):
                    nc.vector.tensor_scalar(wo_sb[:, e], wo_sb[:, e], g_sb[:, e:e + 1], 1.0 - LAMBDA_INIT,
                                            ALU.mult, ALU.mult).then_inc(wog_made, 1)

            def first_body():
                score_max(1, 3, s_score)
                score_max(1, 4, s_score)
                score_max(1, 5, s_score)
                score_max(1, 6, s_score)
                score_max(1, 7, s_score)
                score_max(1, 8, s_score)
                score_max(1, 9, s_score)
                clamp_q(2)
                split_k_0(2)
                score_max(1, 10, s_score)
                score_max(1, 11, s_score)
                score_max(1, 12, s_score)
                combine(0, 0)
                score_max(1, 13, s_score)
                split_k_1(2)
                score_max(1, 14, s_score)
                combine(0, 1)
                energy_max(0)
                normalise(0, 0)
                score_max(1, 15, s_score)
                combine(0, 2)
                cross_weights(0)
                normalise(0, 1)
                split_maxima(1)
                combine(0, 3)
                normalise(0, 2)
                normalise(0, 3)

            def second_body():
                b, t = 1, 0
                score_max(b + 1, 0, s_score)
                score_max(b + 1, 1, s_score)
                score_max(b + 1, 2, s_score)
                score_max(b + 1, 3, s_score)
                first_residual(t)
                score_max(b + 1, 4, s_score)
                score_max(b + 1, 5, s_score)
                layer_norm(t, 0, z, x1, x1_done)
                score_max(b + 1, 6, s_score)
                combine(b, 0)
                second_residual(t)
                score_max(b + 1, 7, s_score)
                layer_norm(t, 1, z, x2, x2_done)
                score_max(b + 1, 8, s_score)
                clamp_q(b + 2)
                split_k_0(b + 2)
                score_max(b + 1, 9, s_score)
                x2T_rest(t)
                gate(t, 0)
                score_max(b + 1, 10, s_score)
                gate(t, 1)
                combine(b, 1)
                score_max(b + 1, 11, s_score)
                split_k_1(b + 2)
                gate(t, 2)
                normalise(b, 0)
                score_max(b + 1, 12, s_score)
                energy_max(b)
                gate(t, 3)
                score_max(b + 1, 13, s_score)
                gate(t, 4)
                combine(b, 2)
                cross_weights(b)
                score_max(b + 1, 14, s_score)
                gate(t, 5)
                normalise(b, 1)
                score_max(b + 1, 15, s_score)
                split_maxima(b + 1)
                gate(t, 6)
                gate(t, 7)
                combine(b, 3)
                normalise(b, 2)
                normalise(b, 3)

            def third_body():
                b, t = 2, 1
                score_max(b + 1, 0, s_score)
                third_residual(t - 1)
                score_max(b + 1, 1, s_score)
                score_max(b + 1, 2, s_score)
                score_max(b + 1, 3, s_score)
                first_residual(t)
                score_max(b + 1, 4, s_score)
                layer_norm(t, 0, z, x1, x1_done)
                score_max(b + 1, 5, s_score)
                score_max(b + 1, 6, s_score)
                combine(b, 0)
                score_max(b + 1, 7, s_score)
                second_residual(t)
                score_max(b + 1, 8, s_score)
                layer_norm(t, 1, z, x2, x2_done)
                third_stats(t - 1)
                score_max(b + 1, 9, s_score)
                x2T_rest(t)
                result(t - 1)
                gate(t, 0)
                combine(b, 1)
                score_max(b + 1, 10, s_score)
                gate(t, 1)
                score_max(b + 1, 11, s_score)
                gate(t, 2)
                score_max(b + 1, 12, s_score)
                gate(t, 3)
                energy_max(b)
                normalise(b, 0)
                score_max(b + 1, 13, s_score)
                gate(t, 4)
                combine(b, 2)
                normalise(b, 1)
                cross_weights(b)
                gate(t, 5)
                score_max(b + 1, 14, s_score)
                score_max(b + 1, 15, s_score)
                split_maxima(b + 1)
                gate(t, 6)
                gate(t, 7)
                combine(b, 3)
                normalise(b, 2)
                normalise(b, 3)

            def last_body():
                b, t = B - 1, B - 2
                third_residual(t - 1)
                first_residual(t)
                layer_norm(t, 0, z, x1, x1_done)
                energy_max(b)
                cross_weights(b)
                second_residual(t)
                layer_norm(t, 1, z, x2, x2_done)
                x2T_rest(t)
                third_stats(t - 1)
                combine(b, 0)
                gate(t, 0)
                result(t - 1)
                gate(t, 1)
                combine(b, 1)
                gate(t, 2)
                gate(t, 3)
                normalise(b, 0)
                gate(t, 4)
                combine(b, 2)
                normalise(b, 1)
                combine(b, 3)
                gate(t, 5)
                normalise(b, 2)
                normalise(b, 3)
                first_residual(b)
                layer_norm(b, 0, z, x1, x1_done)
                gate(t, 6)
                gate(t, 7)
                second_residual(b)
                third_residual(t)
                dve.wait_ge(z3_done, t + 1)
                layer_norm(b, 1, z, x2, x2_done)
                third_stats(t)
                x2T_rest(b)
                result(t)
                gate(b, 0)
                for j in range(1, FB):
                    gate(b, j)
                third_residual(b)
                third_stats(b)
                result(b)

            zeros_in_q(0)
            clamp_q(0)
            dve.wait_ge(v_zeros, 1)
            nc.vector.memset(v_sb[:, :, :, :, DV:DV + 1], 1.0).then_inc(v_ones, 1)
            split_k(0)
            dve.wait_ge(ident_made, 1)
            nc.vector.tensor_copy(ident_bf[:], ident[:]).then_inc(ident_bf_made, 1)
            clamp_q(1)
            zeros_in_q(1)
            dve.wait_ge(loaded["lam"], 16)
            nc.vector.tensor_tensor_reduce(lam_w[:, 0], lam_sb[:, 0], lam_sb[:, 1], 1.0, 0.0, ALU.mult, ALU.add,
                                           lam_d[:, 0:1])
            nc.vector.tensor_tensor_reduce(lam_w[:, 1], lam_sb[:, 2], lam_sb[:, 3], 1.0, 0.0, ALU.mult, ALU.add,
                                           lam_d[:, 1:2]).then_inc(lam_dots, 1)
            for u in range(H):
                if u == SPLIT_AT:
                    split_k(1)
                score_max(0, u, score[u % 2])
            split_maxima(0)
            for u in range(EARLY):
                score_max(1, u, s_score)
            late_constants()
            first_body()
            second_body()
            third_body()
            last_body()


def kernel(x, ctx_1024, L0_attn_Wq, L0_attn_Wk, L0_attn_Wv, L0_attn_Wo, L0_attn_lambda_q1, L0_attn_lambda_k1,
           L0_attn_lambda_q2, L0_attn_lambda_k2, L0_attn_subln_weight, L0_xattn_Wq, L0_xattn_bq, L0_xattn_Wk,
           L0_xattn_bk, L0_ffn_w_gate, L0_ffn_w_up, L0_ffn_w_down):
    import concourse.bacc as bacc
    import numpy as np
    from concourse.bass_utils import run_bass_kernel_spmd

    def rows(a, n):
        a = np.asarray(a)
        return np.ascontiguousarray(a.reshape(n, P, -1).transpose(1, 0, 2))

    def half_heads(w):
        return np.asarray(w).reshape(H, 2, D, E).transpose(1, 2, 0, 3).reshape(E, E)

    x = np.asarray(x)
    context = np.asarray(ctx_1024)
    arrays = {
        "x": np.stack([rows(x[b], TB) for b in range(B)]),
        "xT": np.stack([rows(x[b].T, EB) for b in range(B)]),
        "ctxT": np.ascontiguousarray(context.transpose(0, 2, 1)),
        "wqT": rows(half_heads(L0_attn_Wq).T, EB),
        "wkT": rows(half_heads(L0_attn_Wk).T, EB),
        "wvT": rows(np.asarray(L0_attn_Wv).T, EB),
        "woT": rows(np.asarray(L0_attn_Wo).T, EB),
        "lam_in": np.ascontiguousarray(np.broadcast_to(np.stack([
            np.asarray(a) for a in (L0_attn_lambda_q1, L0_attn_lambda_k1, L0_attn_lambda_q2, L0_attn_lambda_k2)]),
            (P, 4, D))),
        "g_in": np.ascontiguousarray(np.tile(np.asarray(L0_attn_subln_weight), H).reshape(EB, P).T),
        "xwT": np.ascontiguousarray(np.stack([np.asarray(L0_xattn_Wq).T, np.asarray(L0_xattn_Wk).T], 1)),
        "xb": np.ascontiguousarray(np.stack([np.asarray(L0_xattn_bq), np.asarray(L0_xattn_bk)], 1)),
        "wgT": rows(np.asarray(L0_ffn_w_gate).T, EB),
        "wuT": rows(np.asarray(L0_ffn_w_up).T, EB),
        "wdT": rows(np.asarray(L0_ffn_w_down).T, FB),
    }
    nc = bacc.Bacc("TRN2", target_bir_lowering=False, num_devices=1)
    ins = [nc.dram_tensor(n, a.shape, mybir.dt.from_np(a.dtype), kind="ExternalInput").ap() for n, a in arrays.items()]
    out = nc.dram_tensor("out", (B, P, TB, E), F32, kind="ExternalOutput").ap()
    decoder_layer(nc, *ins, out)
    got = run_bass_kernel_spmd(nc, [arrays], core_ids=[0]).results[0]["out"]
    return np.ascontiguousarray(got.transpose(0, 2, 1, 3)).reshape(B, T, E)
```
